# Optimizing a Trainium2 kernel written in Bass

```python
import numpy as np
import jax
import jax.numpy as jnp

def _softmax(x, axis=-1):
    return jax.nn.softmax(x, axis=axis)

def _gelu(x):
    return jax.nn.gelu(x, approximate=True)

def _silu(x):
    return jax.nn.silu(x)

def _sigmoid(x):
    return jax.nn.sigmoid(x)

def _layernorm(x, axis=-1, eps=1e-05):
    m = jnp.mean(x, axis=axis, keepdims=True)
    v = jnp.var(x, axis=axis, keepdims=True)
    return (x - m) / jnp.sqrt(v + eps)

def _scatter_add(tgt, idx, src, axis=0):
    return tgt.at[idx].add(src)

def _segment_sum(src, seg, n):
    return jax.ops.segment_sum(src, seg, n)
kernel_name = 'mk_adj_resnorm_d1_adj_r2_8b65db'

def setup_inputs(seed: int=0):
    np.random.seed(seed)
    _w = jnp.asarray

    def _rec_inputs():
        import jax
        import jax.numpy as jnp
        _gk = jax.random.key(seed)
        x = 7.22e-05 + 1 * jax.random.normal(jax.random.fold_in(_gk, 1), (32, 256, 256), jnp.float32)
        _w = (1.0 + jnp.arange(256, dtype=jnp.float32)) ** (-0.5)
        _w = _w / _w.mean()
        _pij = jnp.clip(0.03125 * _w[:, None] * _w[None, :], 0.0, 1.0)
        _a = jax.random.uniform(jax.random.fold_in(_gk, 2), (256, 256)) < _pij
        adj = _a.astype(jnp.int32)
        return (x, adj)
    x, adj = _rec_inputs()

    def _L0_gnn_setup():
        import jax, jax.numpy as jnp
        import numpy as np
        LEAKY_ALPHA = 0.01
        NEG_INF = -1000000000.0
        LN_EPS = 1e-05

        def _gat_heads(x, adj, W, a):
            O = W.shape[-1]
            Wh = jnp.einsum('bnf,hfo->bhno', x, W)
            f1 = jnp.einsum('bhno,ho->bhn', Wh, a[:, :O])
            f2 = jnp.einsum('bhno,ho->bhn', Wh, a[:, O:])
            e = f1[:, :, :, None] + f2[:, :, None, :]
            e = jnp.where(e > 0, e, LEAKY_ALPHA * e)
            e = jnp.where(adj[None, None] > 0, e, NEG_INF)
            attn = jax.nn.softmax(e, axis=-1)
            return jnp.einsum('bhnm,bhmo->bhno', attn, Wh)
        key = jax.random.key(seed)
        ks = jax.random.split(key, 10)
        B, N, F_in, F_hid, H, F_out, D_ff = (8, 1024, 256, 256, 4, 256, 256)
        s = 0.05
        return {'enc_inputs': jax.random.normal(ks[0], (B, N, F_in), jnp.float32), 'adj': jax.random.randint(ks[1], (N, N), 0, 2, jnp.int32), 'W_heads': jax.random.normal(ks[2], (H, F_in, F_hid), jnp.float32) * s, 'a_heads': jax.random.normal(ks[3], (H, 2 * F_hid), jnp.float32) * s, 'W_out': jax.random.normal(ks[4], (H * F_hid, F_out), jnp.float32) * s, 'a_out': jax.random.normal(ks[5], (2 * F_out,), jnp.float32) * s, 'w1': jax.random.normal(ks[6], (F_out, D_ff), jnp.float32) * s, 'b1': jnp.zeros((D_ff,), jnp.float32), 'w2': jax.random.normal(ks[7], (D_ff, F_out), jnp.float32) * s, 'b2': jnp.zeros((F_out,), jnp.float32), 'ln_gamma': jnp.ones((F_out,), jnp.float32), 'ln_beta': jnp.zeros((F_out,), jnp.float32)}
    _L0_gnn_all = _L0_gnn_setup()
    _L0_gnn_in = {k: v for k, v in _L0_gnn_all.items() if k in ('W_heads', 'a_heads', 'W_out', 'a_out', 'w1', 'b1', 'w2', 'b2', 'ln_gamma', 'ln_beta')}
    del _L0_gnn_all
    return {'x': x, 'adj': adj, 'L0_gnn_W_heads': _L0_gnn_in['W_heads'], 'L0_gnn_a_heads': _L0_gnn_in['a_heads'], 'L0_gnn_W_out': _L0_gnn_in['W_out'], 'L0_gnn_a_out': _L0_gnn_in['a_out'], 'L0_gnn_w1': _L0_gnn_in['w1'], 'L0_gnn_b1': _L0_gnn_in['b1'], 'L0_gnn_w2': _L0_gnn_in['w2'], 'L0_gnn_b2': _L0_gnn_in['b2'], 'L0_gnn_ln_gamma': _L0_gnn_in['ln_gamma'], 'L0_gnn_ln_beta': _L0_gnn_in['ln_beta']}

def reference(x, adj, L0_gnn_W_heads, L0_gnn_a_heads, L0_gnn_W_out, L0_gnn_a_out, L0_gnn_w1, L0_gnn_b1, L0_gnn_w2, L0_gnn_b2, L0_gnn_ln_gamma, L0_gnn_ln_beta):
    import jax
    import jax.numpy as jnp

    def _L0_gnn_ref(enc_inputs, adj, W_heads, a_heads, W_out, a_out, w1, b1, w2, b2, ln_gamma, ln_beta):
        import jax, jax.numpy as jnp
        import numpy as np
        LEAKY_ALPHA = 0.01
        NEG_INF = -1000000000.0
        LN_EPS = 1e-05

        def _gat_heads(x, adj, W, a):
            O = W.shape[-1]
            Wh = jnp.einsum('bnf,hfo->bhno', x, W)
            f1 = jnp.einsum('bhno,ho->bhn', Wh, a[:, :O])
            f2 = jnp.einsum('bhno,ho->bhn', Wh, a[:, O:])
            e = f1[:, :, :, None] + f2[:, :, None, :]
            e = jnp.where(e > 0, e, LEAKY_ALPHA * e)
            e = jnp.where(adj[None, None] > 0, e, NEG_INF)
            attn = jax.nn.softmax(e, axis=-1)
            return jnp.einsum('bhnm,bhmo->bhno', attn, Wh)
        B, N, _ = enc_inputs.shape
        h = jax.nn.elu(_gat_heads(enc_inputs, adj, W_heads, a_heads))
        h = jnp.transpose(h, (0, 2, 1, 3)).reshape(B, N, -1)
        out = _gat_heads(h, adj, W_out[None], a_out[None])[:, 0]
        out = jax.nn.elu(out)
        ffn = jnp.maximum(out @ w1 + b1, 0.0) @ w2 + b2
        y = ffn + out
        mu = jnp.mean(y, axis=-1, keepdims=True)
        var = jnp.var(y, axis=-1, keepdims=True)
        return (y - mu) / jnp.sqrt(var + LN_EPS) * ln_gamma + ln_beta
    x = _layernorm(x + _L0_gnn_ref(x, adj, L0_gnn_W_heads, L0_gnn_a_heads, L0_gnn_W_out, L0_gnn_a_out, L0_gnn_w1, L0_gnn_b1, L0_gnn_w2, L0_gnn_b2, L0_gnn_ln_gamma, L0_gnn_ln_beta), axis=-1)
    return x

_drawn_inputs = setup_inputs


def setup_inputs(seed=0):
    import zlib

    import numpy as np

    out = dict(_drawn_inputs(seed))
    spreads = {'L0_gnn_b1': (0.0, 0.1),
     'L0_gnn_b2': (0.0, 0.1),
     'L0_gnn_ln_gamma': (1.0, 0.2),
     'L0_gnn_ln_beta': (0.0, 0.1)}
    factors = {}
    for name, (base, spread) in spreads.items():
        noise = np.random.default_rng([zlib.crc32(name.encode()), seed]).standard_normal(out[name].shape)
        drawn = base * np.exp(spread * noise) if base else spread * noise
        out[name] = jnp.asarray(drawn.astype(out[name].dtype))
    for name, factor in factors.items():
        out[name] = (out[name] * factor).astype(out[name].dtype)
    return out
```

```python
from contextlib import ExitStack

import concourse.bass as bass
from concourse import mybir

F32 = mybir.dt.float32
F32R = mybir.dt.float32r
BF16 = mybir.dt.bfloat16
I32 = mybir.dt.int32
ACT = mybir.ActivationFunctionType
ALU = mybir.AluOpType
AX = mybir.AxisListType

P = 128
SLOPE = 0.01
MASKED = -1.0e9
EPS = 1e-5


def gat_block(nc: bass.Bass, x, adj, w_heads, a_heads, w_out, a_out, w1, b1, w2, b2, gamma, beta, out):
    B, N, F = x.shape
    H, _, O = w_heads.shape
    PAIRS = B // 2
    NC = N // P
    FC = F // P
    OC = O // P
    KC = H * OC
    FCOLS = 4
    W2N = O + FCOLS
    assert N == F == O == 256 and H == 4 and w_out.shape == (H * O, O) and w1.shape == (O, O)

    ctx = ExitStack()
    with ctx:
        def sb(name, shape, dt):
            return ctx.enter_context(nc.sbuf_tensor(name, shape, dt))

        def sem(name):
            return ctx.enter_context(nc.semaphore(name))

        ident = sb("ident", [P, P], F32)
        ident_b = sb("ident_b", [P, P], BF16)
        ident_r = sb("ident_r", [P, P], F32R)
        ones_r = sb("ones_r", [P, P], F32R)
        adj_i = sb("adj_i", [P, NC, N], I32)
        mask = sb("mask", [P, NC, N], BF16)
        row_sel = sb("row_sel", [P, 3, 8], F32)
        row_w = sb("row_w", [P, 3], F32)
        wh = [sb(f"wh_{s}", [P, FC, H, O], F32R) for s in ("hi", "lo")]
        wo = [sb(f"wo_{s}", [P, KC, W2N], F32R) for s in ("hi", "lo")]
        w1s = [sb(f"w1_{s}", [P, OC, O], F32R) for s in ("hi", "lo")]
        w2s = [sb(f"w2_{s}", [P, OC, O], F32R) for s in ("hi", "lo")]
        u_in = sb("u_in", [P, FC, P], F32)
        u_out = sb("u_out", [P, KC, 2], F32)
        b1c = sb("b1c", [P, OC], F32)
        b2raw = sb("b2raw", [2, O], F32)
        b2h = sb("b2h", [2, O], F32R)
        b2r = sb("b2r", [P, O], F32R)
        gamma_b = sb("gamma_b", [P, O], F32)
        beta_b = sb("beta_b", [P, O], F32)
        eps_c = sb("eps_c", [P, NC], F32)
        minus_half = sb("minus_half", [P, NC], F32)

        xn = sb("xn", [P, 2, NC, F], F32)
        xs = [sb(f"x_{s}", [P, 2, NC, F], F32R) for s in ("hi", "lo")]
        xt = sb("xt", [P, FC, 2, N], F32)
        f_hi = sb("f_hi", [P, 2 * N], F32R)
        f_sp = sb("f_sp", [P, 2 * N], F32R)
        L = sb("L", [P, H, 2 * N], F32R)
        R = sb("R", [P, 2 * N], F32R)
        att = sb("att", [P, 3, 2, NC, N], F32)
        negmax = sb("negmax", [P, 3, 2, NC], F32)
        total = sb("total", [P, 3, 2, NC], F32)
        inv = sb("inv", [P, 3, 2, NC], F32)
        pt = [sb(f"pt_{s}", [P, 2, 2, NC, N], F32R) for s in ("hi", "lo")]
        yt = [sb(f"yt_{s}", [P, 2, FC, 2, N], F32R) for s in ("hi", "lo")]
        elu_w = sb("elu_w", [P, 4, 2 * N], F32)
        ht = [sb(f"ht_{s}", [P, KC, 2 * N], F32R) for s in ("hi", "lo")]
        v = [sb(f"v_{s}", [P, 2, NC, O], F32R) for s in ("hi", "lo")]
        f2pad = sb("f2pad", [P, 2, NC, P], F32)
        L2 = sb("L2", [P, 2 * N], F32R)
        R2 = sb("R2", [P, 2 * N], F32R)
        elu_o = sb("elu_o", [P, OC, 2 * N], F32)
        ot = [sb(f"ot_{s}", [P, OC, 2 * N], F32R) for s in ("hi", "lo")]
        rt = [sb(f"rt_{s}", [P, OC, 2 * N], F32R) for s in ("hi", "lo")]
        xres = sb("xres", [P, 2, NC, O], F32)
        ln = sb("ln", [P, 2, NC, O], F32)
        bn1 = sb("bn1", [P, 2, NC, 6], F32)
        mv1 = sb("mv1", [P, 2, NC, 2], F32)
        ve1 = sb("ve1", [P, 2, NC], F32)
        rs1 = sb("rs1", [P, 2, NC], F32)
        bn2 = sb("bn2", [P, 2, NC, 6], F32)
        mv2 = sb("mv2", [P, 2, NC, 2], F32)
        ve2 = sb("ve2", [P, 2, NC], F32)
        rs2 = sb("rs2", [P, 2, NC], F32)

        bank = [ctx.enter_context(nc.psum_tensor(f"bank{i}", [P, 512], F32)) for i in range(8)]
        ZB, TB, MB = (0, 1), (2, 3), (4, 5, 6, 7)
        BANK = {("xt", b): TB[b] for b in range(2)}
        BANK[("f",)] = ZB[0]
        BANK[("f2",)] = ZB[0]
        for b in range(2):
            for h in range(H + 1):
                BANK[("z", b, h)] = ZB[b]
                BANK[("t", b, h)] = TB[b]
        MAIN = [("v", 0, 0), ("v", 0, 1), ("v", 1, 0), ("v", 1, 1), ("y", 0, 0), ("y", 1, 0), ("y", 0, 1),
                ("w", 0, 0), ("y", 1, 1), ("w", 0, 1), ("o", 0), ("o", 1), ("w", 1, 0), ("w", 1, 1),
                ("y", 0, 2), ("y", 1, 2), ("g", 0), ("g", 1), ("w", 2, 0), ("y", 0, 3), ("w", 2, 1),
                ("y", 1, 3), ("w", 3, 0), ("w", 3, 1), ("r", 0), ("r", 1)]
        for i, tile in enumerate(MAIN):
            BANK[tile] = MB[i % len(MB)]
        TILES = [("xt", 0), ("xt", 1), ("v", 0, 0), ("f",), ("v", 0, 1), ("z", 0, 0), ("z", 1, 0), ("v", 1, 0),
                 ("z", 0, 1), ("v", 1, 1), ("t", 0, 0), ("t", 1, 0), ("z", 1, 1), ("y", 0, 0), ("f2",), ("y", 1, 0),
                 ("t", 0, 1), ("t", 1, 1), ("z", 0, H), ("z", 1, H), ("y", 0, 1), ("w", 0, 0), ("y", 1, 1),
                 ("w", 0, 1), ("z", 0, 2), ("z", 1, 2), ("t", 0, H), ("t", 1, H), ("o", 0), ("o", 1), ("w", 1, 0),
                 ("t", 0, 2), ("t", 1, 2), ("w", 1, 1), ("y", 0, 2), ("y", 1, 2), ("z", 0, 3), ("z", 1, 3),
                 ("g", 0), ("g", 1), ("w", 2, 0), ("t", 0, 3), ("t", 1, 3), ("y", 0, 3), ("w", 2, 1), ("y", 1, 3),
                 ("w", 3, 0), ("w", 3, 1), ("r", 0), ("r", 1)]

        def second(tile):
            return tile[0] in ("v", "f2", "o", "g", "r") or (tile[0] in "zt" and tile[2] == H)

        def reach(eng, s, value):
            if not (isinstance(value, int) and value <= 0):
                eng.wait_ge(s, value)

        def reach_alone(eng, known, *counts):
            for s, n in counts:
                if not isinstance(n, int):
                    eng.compute_val(n)
            eng.wait_ge(*known)
            for s, n in counts:
                reach(eng, s, n)

        def att_slot(h):
            return {0: 0, 1: 1, H: 2, 2: 0, 3: 1}[h]

        def pt_slot(h):
            return {0: 0, 1: 1, H: 0, 2: 1, 3: 0}[h]

        s_wheads, s_wout, s_small, s_adj = sem("s_wheads"), sem("s_wout"), sem("s_small"), sem("s_adj")
        s_consts, s_rowsel, s_setup = sem("s_consts"), sem("s_rowsel"), sem("s_setup")
        dve_chain, pool_chain = sem("dve_chain"), sem("pool_chain")
        weights_split, wheads_used = sem("weights_split"), sem("wheads_used")
        x_loaded = sem("x_loaded")
        xt_ready, xt_copied = sem("xt_ready"), sem("xt_copied")
        x_hi_done, x_lo_done = sem("x_hi_done"), sem("x_lo_done")
        f_ready = [sem("f1_ready"), sem("f2_ready")]
        f_hi_done = [sem("f1_hi_done"), sem("f2_hi_done")]
        f_split = [sem("f1_split"), sem("f2_split")]
        lr_done = [sem("lr1_done"), sem("lr2_done")]
        z_ready = [sem("z1_ready"), sem("z2_ready")]
        relu_done = [sem("relu1_done"), sem("relu2_done")]
        logits_done = [sem("logits1_done"), sem("logits2_done")]
        exp_done = [sem("exp1_done"), sem("exp2_done")]
        inv_done = [sem("inv1_done"), sem("inv2_done")]
        probs_done = [sem("probs1_done"), sem("probs2_done")]
        t_ready = [sem("t1_ready"), sem("t2_ready")]
        pt_hi_done = [sem("pt1_hi_done"), sem("pt2_hi_done")]
        pt_lo_done = [sem("pt1_lo_done"), sem("pt2_lo_done")]
        y_ready, y_hi_done, y_lo_done = sem("y_ready"), sem("y_hi_done"), sem("y_lo_done")
        w_ready = sem("w_ready")
        w_exp, w_neg, w_elu, w_hi, w_lo = (sem(f"w_{s}") for s in ("exp", "neg", "elu", "hi", "lo"))
        v_ready, v_hi, v_lo, f2_cols = (sem(s) for s in ("v_ready", "v_hi_done", "v_lo_done", "f2_cols"))
        o_ready = sem("o_ready")
        o_exp, o_neg, o_elu, o_hi, o_lo = (sem(f"o_{s}") for s in ("exp", "neg", "elu", "hi", "lo"))
        g_ready, g_relu, g_hi, g_lo = (sem(f"g_{s}") for s in ("ready", "relu", "hi", "lo"))
        r_ready = sem("r_ready")
        xres_loaded, xres_ready = sem("xres_loaded"), sem("xres_ready")
        bn1_done, mv1_done, ve1_done, rs1_done = (sem(s) for s in ("bn1_done", "mv1_done", "ve1_done", "rs1_done"))
        scaled, ln1_done = sem("scaled"), sem("ln1_done")
        bn2_done, mv2_done, ve2_done, rs2_done = (sem(s) for s in ("bn2_done", "mv2_done", "ve2_done", "rs2_done"))
        ln2_done = sem("ln2_done")
        stored = sem("stored")

        def item(layer, pair, b, h):
            return pair * (2 * H) + 2 * h + b + 1 if layer == 0 else pair * 2 + b + 1

        def layer_of(h):
            return 1 if h == H else 0

        def read_out(tile, p):
            kind, at = tile[0], tile[1:]
            q = p - 1
            if kind in "zt":
                ly = layer_of(at[1])
                return (logits_done if kind == "z" else pt_lo_done)[ly], item(ly, p - ly, *at)
            if kind == "xt":
                return xt_copied, p * 2 + at[0] + 1
            if kind == "f":
                return f_split[0], p + 1
            if kind == "f2":
                return f_split[1], q + 1
            if kind == "y":
                return y_lo_done, item(0, p, *at)
            if kind == "w":
                return w_elu, p * KC + OC * at[0] + at[1] + 1
            if kind == "v":
                return v_lo, q * 4 + 2 * at[0] + at[1] + 1
            return {"o": o_elu, "g": g_relu, "r": scaled}[kind], q * 2 + at[0] + 1

        def per_step(tile):
            return {"z": 2, "t": 2, "f2": 1, "v": 4, "o": 2, "g": 2, "r": 2}[tile[0]]

        x_rows = x.rearrange("b (c n) f -> n (b c) f", n=P)
        out_rows = out.rearrange("b (c n) f -> n (b c) f", n=P)

        block = ctx.enter_context(nc.Block())

        @block.sync
        def _(sp):
            sp.dma_start(xn[:, :, :, :].rearrange("p b c f -> p (b c) f"), x_rows[:, 0:2 * NC, :]).then_inc(x_loaded, 16)
            raw = att[:, :, :, :, :].rearrange("p s b c m -> p (s b c m)")
            for c in range(FC):
                sp.dma_start(raw[:, c * H * O:(c + 1) * H * O].rearrange("p (h o) -> p h o", h=H),
                             w_heads[:, c * P:(c + 1) * P, :].rearrange("h f o -> f h o")).then_inc(s_wheads, 16)
            sp.dma_start(elu_w[:, :, :].rearrange("p s n -> p (s n)"),
                         a_heads.rearrange("h c -> (h c)").partition_broadcast(P)).then_inc(s_wheads, 16)
            sp.dma_start(adj_i[:, :, :], adj.rearrange("(c n) m -> n c m", n=P)).then_inc(s_adj, 16)
            for i, w in enumerate((w1, w2)):
                sp.dma_start(raw[:, (4 + i) * 512:(5 + i) * 512].rearrange("p (c o) -> p c o", c=OC),
                             w.rearrange("(c p) o -> p c o", p=P)).then_inc(s_small, 16)
            sp.dma_start(b1c[:, :], b1.rearrange("(c p) -> p c", p=P), allow_slow_non_contiguous=True).then_inc(s_small, 16)
            sp.dma_start(b2raw[:, :], b2.partition_broadcast(2)).then_inc(s_small, 16)
            sp.dma_start(gamma_b[:, :], gamma.partition_broadcast(P)).then_inc(s_small, 16)
            sp.dma_start(beta_b[:, :], beta.partition_broadcast(P)).then_inc(s_small, 16)
            sp.dma_start(ln[:, 0, :, :].rearrange("p c o -> p (c o)"), a_out.partition_broadcast(P)).then_inc(s_small, 16)
            sp.wait_ge(wheads_used, 1)
            sp.dma_start(raw[:, 0:KC * O].rearrange("p (k o) -> p k o", k=KC),
                         w_out.rearrange("(k p) o -> p k o", p=P)).then_inc(s_wout, 16)

            def load_next(p):
                reach_alone(sp, (x_loaded, 16), (xt_ready, p * 2 + 2), (x_hi_done, p + 1), (x_lo_done, p + 1))
                sp.dma_start(xn[:, :, :, :].rearrange("p b c f -> p (b c) f"),
                             x_rows[:, bass.ds(p * (2 * NC) + 2 * NC, 2 * NC), :]).then_inc(x_loaded, 16)

            def load_residual(q):
                reach_alone(sp, (x_loaded, 16), (ln1_done, q * 2))
                sp.dma_start(xres[:, :, :, :].rearrange("p b c f -> p (b c) f"),
                             x_rows[:, bass.ds(q * (2 * NC), 2 * NC), :]).then_inc(xres_loaded, 16)

            def store(q):
                for b in range(2):
                    reach_alone(sp, (x_loaded, 16), (ln2_done, q * 2 + b + 1))
                    sp.dma_start(out_rows[:, bass.ds(q * (2 * NC) + b * NC, NC), :], ln[:, b, :, :]).then_inc(stored, 16)

            load_next(0)
            load_residual(0)
            load_next(1)
            store(0)
            with sp.Fori(2, PAIRS - 1) as p:
                load_residual(p - 1)
                load_next(p)
                store(p - 1)
            for p in (PAIRS - 1, PAIRS):
                load_residual(p - 1)
                store(p - 1)
            sp.wait_ge(stored, PAIRS * 32)

        @block.gpsimd
        def _(pool):
            def link(ins, n):
                ins.then_inc(pool_chain, 1)
                pool.wait_ge(pool_chain, n)

            link(nc.gpsimd.memset(ident[:, :], 0.0), 1)
            link(nc.gpsimd.affine_select(out=ident[:, :], in_=ident[:, :], compare_op=ALU.not_equal, fill=1.0,
                                         base=0, pattern=[[-1, P]], channel_multiplier=1), 2)
            link(nc.gpsimd.memset(row_sel[:, :, :], 0.0), 3)
            n = 3
            for kind, off in ((0, 0), (0, 1), (1, 2), (1, 3)):
                n += 1
                sel = row_sel[:, kind, 0:H]
                link(nc.gpsimd.affine_select(out=sel, in_=sel, compare_op=ALU.not_equal, fill=1.0,
                                             base=-off, pattern=[[-4, H]], channel_multiplier=1), n)
            sel = row_sel[:, 2, :]
            link(nc.gpsimd.affine_select(out=sel, in_=sel, compare_op=ALU.not_equal, fill=-1.0,
                                         base=-1, pattern=[[-2, 2 * H]], channel_multiplier=1), n + 1)
            nc.gpsimd.memset(eps_c[:, :], EPS)
            nc.gpsimd.memset(minus_half[:, :], -0.5).then_inc(s_consts, 1)

            def x_lo(p):
                pool.wait_ge(x_hi_done, p + 1)
                nc.gpsimd.tensor_tensor(xs[1][:, :, :, :], xn[:, :, :, :], xs[0][:, :, :, :],
                                        ALU.subtract).then_inc(x_lo_done, 1)

            def h_lo(p, h, oc):
                pool.wait_ge(w_hi, p * KC + OC * h + oc + 1)
                s = (OC * h + oc) % 4
                nc.gpsimd.tensor_tensor(ht[1][:, OC * h + oc, :], elu_w[:, s, :], ht[0][:, OC * h + oc, :],
                                        ALU.subtract).then_inc(w_lo, 1)

            def residual(q):
                pool.wait_ge(xres_loaded, q * 16 + 16)
                nc.gpsimd.tensor_tensor(xres[:, :, :, :].rearrange("p b c o -> p (b c) o"),
                                        xres[:, :, :, :].rearrange("p b c o -> p (b c) o"),
                                        beta_b[:, :].unsqueeze(1).broadcast_to([P, 2 * NC, O]),
                                        ALU.add).then_inc(xres_ready, 1)

            def o_lo_(q, oc):
                pool.wait_ge(o_hi, q * 2 + oc + 1)
                nc.gpsimd.tensor_tensor(ot[1][:, oc, :], elu_o[:, oc, :], ot[0][:, oc, :],
                                        ALU.subtract).then_inc(o_lo, 1)

            def r_lo_(q, dc):
                pool.wait_ge(g_hi, q * 2 + dc + 1)
                nc.gpsimd.tensor_tensor(rt[1][:, dc, :], elu_o[:, dc, :], rt[0][:, dc, :],
                                        ALU.subtract).then_inc(g_lo, 1)

            def rstd(q, b, mv, ve, rs, mv_done, ve_done, rs_done):
                pool.wait_ge(mv_done, q * 2 + b + 1)
                nc.gpsimd.tensor_tensor(ve[:, b, :], mv[:, b, :, 1], eps_c[:, :], ALU.add).then_inc(ve_done, 1)
                pool.wait_ge(ve_done, q * 2 + b + 1)
                nc.gpsimd.tensor_tensor(rs[:, b, :], ve[:, b, :], minus_half[:, :], ALU.pow).then_inc(rs_done, 1)

            def rstd1(q, b):
                rstd(q, b, mv1, ve1, rs1, mv1_done, ve1_done, rs1_done)

            def rstd2(q, b):
                rstd(q, b, mv2, ve2, rs2, mv2_done, ve2_done, rs2_done)

            def step(p, one, two):
                q = p - 1
                if one:
                    x_lo(p)
                if two:
                    residual(q)
                if one:
                    h_lo(p, 0, 0), h_lo(p, 0, 1)
                if two:
                    o_lo_(q, 0), o_lo_(q, 1)
                if one:
                    h_lo(p, 1, 0), h_lo(p, 1, 1)
                if two:
                    r_lo_(q, 0), r_lo_(q, 1)
                if one:
                    h_lo(p, 2, 0), h_lo(p, 2, 1)
                    h_lo(p, 3, 0), h_lo(p, 3, 1)
                if two:
                    rstd1(q, 0), rstd1(q, 1)
                    rstd2(q, 0), rstd2(q, 1)

            step(0, True, False)
            step(1, True, True)
            with pool.Fori(2, PAIRS) as p:
                step(p, True, True)
            step(PAIRS, False, True)

        @block.tensor
        def _(pe):
            held, order = {}, []

            def take(tile, p):
                b = BANK[tile]
                if b in held:
                    pe.wait_ge(*read_out(held[b], p))
                elif not (isinstance(p, int) and p == 0):
                    there = [t for t in TILES if BANK[t] == b]
                    firsts = [t for t in there if not second(t)]
                    seconds = [t for t in there if second(t)]
                    if firsts:
                        pe.wait_ge(*read_out(firsts[-1], p - 1))
                    if seconds:
                        s = read_out(seconds[-1], p)[0]
                        pe.wait_ge(s, (p - 1) * per_step(seconds[-1]))
                held[b] = tile
                order.append(tile)
                return bank[b]

            def split_product(ps, lhs, rhs, n, start=True, last_stop=True):
                for i in range(n):
                    for j, (a, b) in enumerate(((0, 0), (1, 0), (0, 1))):
                        mm = nc.tensor.matmul(ps, lhs(a, i), rhs(b, i), start=(start and i == 0 and j == 0),
                                              stop=(last_stop and i == n - 1 and j == 2))
                return mm

            def transpose_x(p, b):
                ps = take(("xt", b), p)
                if b == 0:
                    pe.wait_ge(x_loaded, p * 16 + 16)
                for fc in range(FC):
                    for c in range(NC):
                        mm = nc.tensor.transpose(ps[:, fc * N + c * P:fc * N + (c + 1) * P],
                                                 xn[:, b, c, fc * P:(fc + 1) * P], ident[:, :])
                mm.then_inc(xt_ready, 1)

            def f_rows(p):
                ps = take(("f",), p)
                pe.wait_ge(xt_copied, p * 2 + 2)
                for fc in range(FC):
                    mm = nc.tensor.matmul(ps[:, :], u_in[:, fc, :], xt[:, fc, :, :].rearrange("p b n -> p (b n)"),
                                          start=(fc == 0), stop=(fc == FC - 1))
                mm.then_inc(f_ready[0], 1)

            def f2_rows(p):
                ps = take(("f2",), p)
                pe.wait_ge(f2_cols, (p - 1) * 4 + 4)
                for b in range(2):
                    for c in range(NC):
                        mm = nc.tensor.transpose(ps[:, b * N + c * P:b * N + (c + 1) * P], f2pad[:, b, c, :], ident[:, :])
                mm.then_inc(f_ready[1], 1)

            def scores(p, b, h):
                ps = take(("z", b, h), p)
                ly = layer_of(h)
                pe.wait_ge(lr_done[ly], p - ly + 1)
                lhs, rhs = (L[:, h, :], R) if ly == 0 else (L2, R2)
                for c in range(NC):
                    region = ps[:, c * N:(c + 1) * N]
                    nc.tensor.matmul(region, ident_b[:, :], mask[:, c, :], start=True, stop=False)
                    mm = nc.tensor.matmul(region, lhs[:, b * N + c * P:b * N + (c + 1) * P], rhs[:, b * N:(b + 1) * N],
                                          start=False, stop=True)
                mm.then_inc(z_ready[ly], 1)

            def transpose_probs(p, b, h):
                ps = take(("t", b, h), p)
                ly = layer_of(h)
                pe.wait_ge(probs_done[ly], item(ly, p - ly, b, h))
                for mc in range(NC):
                    for c in range(NC):
                        mm = nc.tensor.transpose(ps[:, mc * N + c * P:mc * N + (c + 1) * P],
                                                 att[:, att_slot(h), b, c, mc * P:(mc + 1) * P], ident[:, :])
                mm.then_inc(t_ready[ly], 1)

            def attend_x(p, b, h):
                ps = take(("y", b, h), p)
                pe.wait_ge(pt_hi_done[0], item(0, p, b, h))
                pe.wait_ge(pt_lo_done[0], item(0, p, b, h))
                if h == 0 and b == 0:
                    pe.wait_ge(x_lo_done, p + 1)
                for fc in range(FC):
                    mm = split_product(ps[:, fc * N:(fc + 1) * N],
                                       lambda s, i: xs[s][:, b, i, fc * P:(fc + 1) * P],
                                       lambda s, i: pt[s][:, pt_slot(h), b, i, :], NC)
                mm.then_inc(y_ready, 1)

            def project_head(p, h, oc):
                ps = take(("w", h, oc), p)
                pe.wait_ge(y_hi_done, item(0, p, 1, h))
                pe.wait_ge(y_lo_done, item(0, p, 1, h))
                split_product(ps[:, :], lambda s, i: wh[s][:, i, h, oc * P:(oc + 1) * P],
                              lambda s, i: yt[s][:, h % 2, i, :, :].rearrange("p b n -> p (b n)"),
                              FC).then_inc(w_ready, 1)

            def project_out(p, b, mc):
                ps = take(("v", b, mc), p)
                for k in range(KC):
                    pe.wait_ge(w_lo, (p - 1) * KC + k + 1)
                    for j, (s, t) in enumerate(((0, 0), (1, 0), (0, 1))):
                        mm = nc.tensor.matmul(ps[:, 0:W2N], ht[s][:, k, b * N + mc * P:b * N + (mc + 1) * P],
                                              wo[t][:, k, :], start=(k == 0 and j == 0), stop=(k == KC - 1 and j == 2))
                mm.then_inc(v_ready, 1)

            def attend_out(p, oc):
                ps = take(("o", oc), p)
                q = p - 1
                pe.wait_ge(v_lo, q * 4 + 4)
                for b in range(2):
                    pe.wait_ge(pt_hi_done[1], item(1, q, b, H))
                    pe.wait_ge(pt_lo_done[1], item(1, q, b, H))
                    mm = split_product(ps[:, b * N:(b + 1) * N],
                                       lambda s, i: v[s][:, b, i, oc * P:(oc + 1) * P],
                                       lambda s, i: pt[s][:, pt_slot(H), b, i, :], NC)
                mm.then_inc(o_ready, 1)

            def ffn_in(p, dc):
                ps = take(("g", dc), p)
                pe.wait_ge(o_lo, (p - 1) * 2 + 2)
                split_product(ps[:, :], lambda s, i: w1s[s][:, i, dc * P:(dc + 1) * P],
                              lambda s, i: ot[s][:, i, :], OC).then_inc(g_ready, 1)

            def ffn_out(p, b):
                ps = take(("r", b), p)
                pe.wait_ge(g_lo, (p - 1) * 2 + 2)
                for c in range(NC):
                    cols = slice(b * N + c * P, b * N + (c + 1) * P)
                    nc.tensor.matmul(ps[:, c * O:(c + 1) * O], ones_r[:, :], b2r[:, :], start=True, stop=False)
                    split_product(ps[:, c * O:(c + 1) * O], lambda s, i: rt[s][:, i, cols],
                                  lambda s, i: w2s[s][:, i, :], OC, start=False, last_stop=False)
                    for oc in range(OC):
                        for s in range(2):
                            mm = nc.tensor.matmul(ps[:, c * O + oc * P:c * O + (oc + 1) * P], ot[s][:, oc, cols],
                                                  ident_r[:, :], start=False, stop=(oc == OC - 1 and s == 1))
                mm.then_inc(r_ready, 1)

            def step(p, one, two):
                held.clear()
                order.clear()
                if one:
                    transpose_x(p, 0), transpose_x(p, 1)
                if two:
                    project_out(p, 0, 0)
                if one:
                    f_rows(p)
                if two:
                    project_out(p, 0, 1)
                if one:
                    scores(p, 0, 0), scores(p, 1, 0)
                if two:
                    project_out(p, 1, 0)
                if one:
                    scores(p, 0, 1)
                if two:
                    project_out(p, 1, 1)
                if one:
                    transpose_probs(p, 0, 0), transpose_probs(p, 1, 0)
                    scores(p, 1, 1)
                    attend_x(p, 0, 0)
                if two:
                    f2_rows(p)
                if one:
                    attend_x(p, 1, 0)
                    transpose_probs(p, 0, 1), transpose_probs(p, 1, 1)
                if two:
                    scores(p, 0, H), scores(p, 1, H)
                if one:
                    attend_x(p, 0, 1)
                    project_head(p, 0, 0)
                    attend_x(p, 1, 1)
                    project_head(p, 0, 1)
                    scores(p, 0, 2), scores(p, 1, 2)
                if two:
                    transpose_probs(p, 0, H), transpose_probs(p, 1, H)
                    attend_out(p, 0), attend_out(p, 1)
                if one:
                    project_head(p, 1, 0)
                    transpose_probs(p, 0, 2), transpose_probs(p, 1, 2)
                    project_head(p, 1, 1)
                    attend_x(p, 0, 2), attend_x(p, 1, 2)
                    scores(p, 0, 3), scores(p, 1, 3)
                if two:
                    ffn_in(p, 0), ffn_in(p, 1)
                if one:
                    project_head(p, 2, 0)
                    transpose_probs(p, 0, 3), transpose_probs(p, 1, 3)
                    attend_x(p, 0, 3)
                    project_head(p, 2, 1)
                    attend_x(p, 1, 3)
                    project_head(p, 3, 0), project_head(p, 3, 1)
                if two:
                    ffn_out(p, 0), ffn_out(p, 1)

            pe.wait_ge(s_setup, 1)
            step(0, True, False)
            step(1, True, True)
            with pe.Fori(2, PAIRS) as p:
                step(p, True, True)
            assert order == TILES
            step(PAIRS, False, True)

        @block.scalar
        def _(act):
            def split_f(p, ly):
                ps = bank[BANK[("f",) if ly == 0 else ("f2",)]]
                act.wait_ge(f_ready[ly], p - ly + 1)
                rows = P if ly == 0 else 4
                if ly == 0:
                    reach(act, f_split[1], p - 1)
                    reach(act, f_split[0], p)
                else:
                    act.wait_ge(f_split[0], p + 1 if one_now[0] else PAIRS)
                nc.scalar.activation(f_hi[0:rows, :], ps[0:rows, :], ACT.Copy).then_inc(f_hi_done[ly], 1)

            def relu_part(p, b, h):
                ly = layer_of(h)
                n = item(ly, p - ly, b, h)
                act.wait_ge(z_ready[ly], n)
                if h == H:
                    reach(act, t_ready[1], (p - 1) * 2)
                else:
                    reach(act, t_ready[0], item(0, p - 1, b, h + 2) if h < 2 else item(0, p, b, h - 2))
                nc.scalar.activation(att[:, att_slot(h), b, :, :].rearrange("p c m -> p (c m)"),
                                     bank[BANK[("z", b, h)]][:, :], ACT.Relu,
                                     scale=(1.0 - SLOPE) / SLOPE).then_inc(relu_done[ly], 1)

            def exps(p, b, h):
                ly, s = layer_of(h), att_slot(h)
                n = item(ly, p - ly, b, h)
                act.wait_ge(logits_done[ly], n)
                for c in range(NC):
                    ins = nc.scalar.activation(att[:, s, b, c, :], att[:, s, b, c, :], ACT.Exp, scale=-1.0,
                                               bias=negmax[:, s, b, c:c + 1], accum_out=total[:, s, b, c:c + 1])
                ins.then_inc(exp_done[ly], 1)

            def pt_hi(p, b, h):
                ly = layer_of(h)
                act.wait_ge(t_ready[ly], item(ly, p - ly, b, h))
                if h in (0, 2):
                    reach(act, y_ready, item(0, p - 1, b, 3) if h == 0 else item(0, p, b, 1))
                elif h == 1:
                    reach(act, y_ready, item(0, p - 1, b, 2))
                elif h == H:
                    reach(act, y_ready, item(0, p, b, 0) if one_now[0] else PAIRS * 2 * H)
                elif two_now[0]:
                    act.wait_ge(o_ready, (p - 1) * 2 + 2)
                else:
                    act.wait_ge(y_ready, item(0, p, b, 0))
                nc.scalar.activation(pt[0][:, pt_slot(h), b, :, :].rearrange("p c n -> p (c n)"),
                                     bank[BANK[("t", b, h)]][:, :], ACT.Copy).then_inc(pt_hi_done[ly], 1)

            def y_hi(p, b, h):
                act.wait_ge(y_ready, item(0, p, b, h))
                reach(act, w_ready, p * KC + OC * (h - 1) if h >= 2 else p * KC - KC + OC * (h + 3))
                nc.scalar.activation(yt[0][:, h % 2, :, b, :], bank[BANK[("y", b, h)]][:, :].rearrange(
                    "p (c n) -> p c n", c=FC), ACT.Copy).then_inc(y_hi_done, 1)

            def elu_parts(p, h, oc):
                i = OC * h + oc
                act.wait_ge(w_ready, p * KC + i + 1)
                reach(act, w_lo, p * KC + i + 1 - 4)
                nc.scalar.activation(elu_w[:, i % 4, :], bank[BANK[("w", h, oc)]][:, :], ACT.Exp).then_inc(w_exp, 1)
                act.wait_ge(w_exp, p * KC + i + 1)
                nc.scalar.activation(elu_w[:, i % 4, :], elu_w[:, i % 4, :], ACT.Relu, scale=-1.0,
                                     bias=1.0).then_inc(w_neg, 1)

            def v_hi_(p, b, mc):
                q = p - 1
                i = 2 * b + mc
                act.wait_ge(v_ready, q * 4 + i + 1)
                reach(act, o_ready, q * 2)
                reach(act, f_ready[1], q)
                ps = bank[BANK[("v", b, mc)]]
                nc.scalar.activation(v[0][:, b, mc, :], ps[:, 0:O], ACT.Copy).then_inc(v_hi, 1)
                nc.scalar.activation(f2pad[:, b, mc, 0:FCOLS], ps[:, O:W2N], ACT.Copy).then_inc(f2_cols, 1)

            def elu_out_parts(p, oc):
                q = p - 1
                act.wait_ge(o_ready, q * 2 + oc + 1)
                reach(act, g_lo, q * 2)
                nc.scalar.activation(elu_o[:, oc, :], bank[BANK[("o", oc)]][:, :], ACT.Exp).then_inc(o_exp, 1)
                act.wait_ge(o_exp, q * 2 + oc + 1)
                nc.scalar.activation(elu_o[:, oc, :], elu_o[:, oc, :], ACT.Relu, scale=-1.0, bias=1.0).then_inc(o_neg, 1)

            def ffn_relu(p, dc):
                q = p - 1
                act.wait_ge(g_ready, q * 2 + dc + 1)
                ins = nc.scalar.activation(elu_o[:, dc, :], bank[BANK[("g", dc)]][:, :], ACT.Relu, bias=b1c[:, dc:dc + 1])
                ins.then_inc(g_relu, 1)

            one_now, two_now = [True], [True]

            def step(p, one, two):
                one_now[0], two_now[0] = one, two
                if two:
                    v_hi_(p, 0, 0)
                if one:
                    split_f(p, 0)
                if two:
                    v_hi_(p, 0, 1)
                if one:
                    relu_part(p, 0, 0), relu_part(p, 1, 0)
                    exps(p, 0, 0), exps(p, 1, 0)
                if two:
                    v_hi_(p, 1, 0)
                if one:
                    relu_part(p, 0, 1)
                    exps(p, 0, 1)
                if two:
                    v_hi_(p, 1, 1)
                if one:
                    pt_hi(p, 0, 0), pt_hi(p, 1, 0)
                    relu_part(p, 1, 1)
                    exps(p, 1, 1)
                if two:
                    split_f(p, 1)
                if one:
                    y_hi(p, 0, 0)
                    pt_hi(p, 0, 1)
                    y_hi(p, 1, 0)
                    pt_hi(p, 1, 1)
                if two:
                    relu_part(p, 0, H), relu_part(p, 1, H)
                    exps(p, 0, H)
                if one:
                    y_hi(p, 0, 1)
                if two:
                    exps(p, 1, H)
                if one:
                    elu_parts(p, 0, 0)
                    y_hi(p, 1, 1)
                    relu_part(p, 0, 2)
                    elu_parts(p, 0, 1)
                    relu_part(p, 1, 2)
                    exps(p, 0, 2)
                if two:
                    pt_hi(p, 0, H), pt_hi(p, 1, H)
                if one:
                    exps(p, 1, 2)
                if two:
                    elu_out_parts(p, 0)
                if one:
                    elu_parts(p, 1, 0)
                if two:
                    elu_out_parts(p, 1)
                if one:
                    pt_hi(p, 0, 2), pt_hi(p, 1, 2)
                    elu_parts(p, 1, 1)
                    y_hi(p, 0, 2), y_hi(p, 1, 2)
                    relu_part(p, 0, 3), relu_part(p, 1, 3)
                    exps(p, 0, 3), exps(p, 1, 3)
                if two:
                    ffn_relu(p, 0), ffn_relu(p, 1)
                if one:
                    elu_parts(p, 2, 0)
                    pt_hi(p, 0, 3), pt_hi(p, 1, 3)
                    y_hi(p, 0, 3)
                    elu_parts(p, 2, 1)
                    y_hi(p, 1, 3)
                    elu_parts(p, 3, 0), elu_parts(p, 3, 1)

            step(0, True, False)
            step(1, True, True)
            with act.Fori(2, PAIRS) as p:
                step(p, True, True)
            step(PAIRS, False, True)

        @block.vector
        def _(dve):
            chain = [0]

            def link(ins):
                chain[0] += 1
                ins.then_inc(dve_chain, 1)
                dve.wait_ge(dve_chain, chain[0])

            def set_up():
                for t in (L2, R2, b2r):
                    link(nc.vector.memset(t[:, :].bitcast(F32), 0.0))
                link(nc.vector.memset(ones_r[:, :].bitcast(F32), 1.0))
                link(nc.vector.memset(f2pad[:, :, :, :], 0.0))
                link(nc.vector.memset(u_in[:, :, :], 0.0))
                dve.wait_ge(s_consts, 1)
                link(nc.vector.tensor_copy(ident_b[:, :], ident[:, :]))
                link(nc.vector.tensor_copy(ident_r[:, :], ident[:, :]))
                link(nc.vector.tensor_reduce(row_w[:, :], row_sel[:, :, :], AX.X, ALU.add))
                dve.wait_ge(s_adj, 16)
                link(nc.vector.tensor_scalar(mask[:, :, :], adj_i[:, :, :], 0.0, MASKED, ALU.is_le, ALU.mult))
                raw = att[:, :, :, :, :].rearrange("p s b c m -> p (s b c m)")
                junk = xt[:, 0, 0, :]
                dve.wait_ge(s_wheads, 16 * (FC + 1))
                flat = [w[:, :, :, :].rearrange("p c h o -> p (c h o)") for w in wh]
                link(nc.vector.tensor_copy(flat[0], raw[:, 0:FC * H * O]))
                link(nc.vector.tensor_tensor(flat[1], raw[:, 0:FC * H * O], flat[0], ALU.subtract))
                a_in = elu_w[:, :, :].rearrange("p s n -> p (s n)")
                for c in range(FC):
                    for i in range(2 * H):
                        link(nc.vector.tensor_tensor_reduce(
                            junk, raw[:, (c * H + i // 2) * O:(c * H + i // 2 + 1) * O], a_in[:, i * O:(i + 1) * O],
                            SLOPE, 0.0, ALU.mult, ALU.add, u_in[:, c, 2 * i:2 * i + 1]))
                pairs = u_in[:, :, 0:4 * H].rearrange("p c (i e) -> p c i e", e=2)
                link(nc.vector.tensor_copy(pairs[:, :, :, 1], pairs[:, :, :, 0]))
                nc.vector.memset(row_sel[:, 2, 0:1], 0.0).then_inc(wheads_used, 1)
                dve.wait_ge(s_small, 16 * 7)
                for i, w in enumerate((w1s, w2s)):
                    part = [t[:, :, :].rearrange("p c o -> p (c o)") for t in w]
                    link(nc.vector.tensor_copy(part[0], raw[:, (4 + i) * 512:(5 + i) * 512]))
                    link(nc.vector.tensor_tensor(part[1], raw[:, (4 + i) * 512:(5 + i) * 512], part[0], ALU.subtract))
                link(nc.vector.tensor_copy(b2h[:, :], b2raw[:, :]))
                link(nc.vector.scalar_tensor_tensor(out=b2r[0:2, :], in0=b2h[:, :], scalar=row_w[0:2, 2:3],
                                                    in1=b2raw[:, :], op0=ALU.mult, op1=ALU.add))
                dve.wait_ge(s_wout, 16)
                raw_o = raw[:, 0:KC * O].rearrange("p (k o) -> p k o", k=KC)
                link(nc.vector.tensor_copy(wo[0][:, :, 0:O], raw_o))
                link(nc.vector.tensor_tensor(wo[1][:, :, 0:O], raw_o, wo[0][:, :, 0:O], ALU.subtract))
                a_o = ln[:, 0, :, :]
                for k in range(KC):
                    for j in range(2):
                        link(nc.vector.tensor_tensor_reduce(junk, raw_o[:, k, :], a_o[:, j, :], SLOPE, 0.0,
                                                            ALU.mult, ALU.add, u_out[:, k, j:j + 1]))
                cols = [w[:, :, O:W2N].rearrange("p k (j e) -> p k j e", e=2) for w in wo]
                for e in range(2):
                    link(nc.vector.tensor_copy(cols[0][:, :, :, e], u_out[:, :, :]))
                    link(nc.vector.tensor_tensor(cols[1][:, :, :, e], u_out[:, :, :], cols[0][:, :, :, e], ALU.subtract))
                nc.vector.memset(row_sel[:, 2, 1:2], 0.0).then_inc(s_setup, 1)

            def copy_xt(p, b):
                dve.wait_ge(xt_ready, p * 2 + b + 1)
                reach(dve, f_ready[0], p)
                nc.vector.tensor_copy(xt[:, :, b, :], bank[TB[b]][:, :].rearrange("p (c n) -> p c n", c=FC)).then_inc(xt_copied, 1)

            def x_hi(p):
                dve.wait_ge(x_loaded, p * 16 + 16)
                reach(dve, y_ready, p * 2 * H)
                nc.vector.tensor_copy(xs[0][:, :, :, :].rearrange("p b c f -> p (b c f)"),
                                      xn[:, :, :, :].rearrange("p b c f -> p (b c f)")).then_inc(x_hi_done, 1)

            def factors(p, ly):
                q = p - ly
                rows = P if ly == 0 else 4
                tile = ("f",) if ly == 0 else ("f2",)
                ps = bank[BANK[tile]]
                dve.wait_ge(f_hi_done[ly], q + 1)
                if ly == 0:
                    reach(dve, lr_done[1], p - 1)
                    reach(dve, lr_done[0], p)
                else:
                    dve.wait_ge(lr_done[0], p + 1 if one_now[0] else PAIRS)
                nc.vector.scalar_tensor_tensor(out=f_sp[0:rows, :], in0=f_hi[0:rows, :], scalar=row_w[0:rows, 2:3],
                                               in1=ps[0:rows, :], op0=ALU.mult, op1=ALU.add).then_inc(f_split[ly], 1)
                dve.wait_ge(f_split[ly], q + 1)
                reach(dve, z_ready[ly], q * 2 * H if ly == 0 else q * 2)
                if ly == 0:
                    for h in range(H):
                        nc.vector.tensor_scalar(L[:, h, :], f_sp[:, :], row_sel[:, 0, h:h + 1],
                                                row_sel[:, 1, h:h + 1], ALU.mult, ALU.add)
                    nc.vector.tensor_scalar(R[:, :], f_sp[:, :], row_w[:, 1:2], row_w[:, 0:1], ALU.mult,
                                            ALU.add).then_inc(lr_done[0], 1)
                else:
                    nc.vector.tensor_scalar(L2[0:4, :], f_sp[0:4, :], row_sel[0:4, 0, 0:1], row_sel[0:4, 1, 0:1],
                                            ALU.mult, ALU.add)
                    nc.vector.tensor_scalar(R2[0:4, :], f_sp[0:4, :], row_w[0:4, 1:2], row_w[0:4, 0:1], ALU.mult,
                                            ALU.add).then_inc(lr_done[1], 1)

            def logits(p, b, h):
                ly, s = layer_of(h), att_slot(h)
                reach_alone(dve, (s_setup, 1), (relu_done[ly], item(ly, p - ly, b, h)))
                ps = bank[BANK[("z", b, h)]]
                for c in range(NC):
                    ins = nc.vector.tensor_tensor_reduce(att[:, s, b, c, :], ps[:, c * N:(c + 1) * N],
                                                         att[:, s, b, c, :], -1.0, 3.0e38, ALU.add, ALU.min,
                                                         negmax[:, s, b, c:c + 1])
                ins.then_inc(logits_done[ly], 1)

            def normalize(p, b, h):
                ly, s = layer_of(h), att_slot(h)
                n = item(ly, p - ly, b, h)
                dve.wait_ge(exp_done[ly], n)
                nc.vector.reciprocal(inv[:, s, b, :], total[:, s, b, :]).then_inc(inv_done[ly], 1)
                dve.wait_ge(inv_done[ly], n)
                for c in range(NC):
                    ins = nc.vector.tensor_scalar(att[:, s, b, c, :], att[:, s, b, c, :], inv[:, s, b, c:c + 1], None,
                                                  ALU.mult)
                ins.then_inc(probs_done[ly], 1)

            def pt_lo(p, b, h):
                ly = layer_of(h)
                dve.wait_ge(pt_hi_done[ly], item(ly, p - ly, b, h))
                dst = [t[:, pt_slot(h), b, :, :].rearrange("p c n -> p (c n)") for t in pt]
                nc.vector.tensor_tensor(dst[1], bank[BANK[("t", b, h)]][:, :], dst[0], ALU.subtract).then_inc(pt_lo_done[ly], 1)

            def y_lo(p, b, h):
                dve.wait_ge(y_hi_done, item(0, p, b, h))
                nc.vector.tensor_tensor(yt[1][:, h % 2, :, b, :], bank[BANK[("y", b, h)]][:, :].rearrange(
                    "p (c n) -> p c n", c=FC), yt[0][:, h % 2, :, b, :], ALU.subtract).then_inc(y_lo_done, 1)

            def elu(p, h, oc):
                i = OC * h + oc
                dve.wait_ge(w_neg, p * KC + i + 1)
                nc.vector.scalar_tensor_tensor(out=elu_w[:, i % 4, :], in0=bank[BANK[("w", h, oc)]][:, :], scalar=0.0,
                                               in1=elu_w[:, i % 4, :], op0=ALU.max, op1=ALU.subtract).then_inc(w_elu, 1)
                dve.wait_ge(w_elu, p * KC + i + 1)
                if i == 0:
                    reach(dve, v_ready, p * 4)
                nc.vector.tensor_copy(ht[0][:, i, :], elu_w[:, i % 4, :]).then_inc(w_hi, 1)

            def v_lo_(p, b, mc):
                dve.wait_ge(v_hi, (p - 1) * 4 + 2 * b + mc + 1)
                dve.wait_ge(f2_cols, (p - 1) * 4 + 2 * b + mc + 1)
                nc.vector.tensor_tensor(v[1][:, b, mc, :], bank[BANK[("v", b, mc)]][:, 0:O], v[0][:, b, mc, :],
                                        ALU.subtract).then_inc(v_lo, 1)

            def elu_out(p, oc):
                q = p - 1
                dve.wait_ge(o_neg, q * 2 + oc + 1)
                nc.vector.scalar_tensor_tensor(out=elu_o[:, oc, :], in0=bank[BANK[("o", oc)]][:, :], scalar=0.0,
                                               in1=elu_o[:, oc, :], op0=ALU.max, op1=ALU.subtract).then_inc(o_elu, 1)
                dve.wait_ge(o_elu, q * 2 + oc + 1)
                reach(dve, r_ready, q * 2)
                nc.vector.tensor_copy(ot[0][:, oc, :], elu_o[:, oc, :]).then_inc(o_hi, 1)

            def ffn_hi(p, dc):
                q = p - 1
                dve.wait_ge(g_relu, q * 2 + dc + 1)
                nc.vector.tensor_copy(rt[0][:, dc, :], elu_o[:, dc, :]).then_inc(g_hi, 1)

            def norm_stats(p, b):
                q = p - 1
                n = q * 2 + b + 1
                ps = bank[BANK[("r", b)]]
                dve.wait_ge(r_ready, n)
                for c in range(NC):
                    ins = nc.vector.bn_stats(bn1[:, b, c, :], ps[:, c * O:(c + 1) * O])
                ins.then_inc(bn1_done, 1)
                reach_alone(dve, (s_setup, 1), (bn1_done, n))
                for c in range(NC):
                    ins = nc.vector.bn_aggr(mv1[:, b, c, :], bn1[:, b, c, :])
                ins.then_inc(mv1_done, 1)
                dve.wait_ge(mv1_done, n)
                reach(dve, stored, q * 32)
                for c in range(NC):
                    ins = nc.vector.scalar_tensor_tensor(out=ln[:, b, c, :], in0=ps[:, c * O:(c + 1) * O],
                                                         scalar=mv1[:, b, c, 0:1], in1=gamma_b[:, :],
                                                         op0=ALU.subtract, op1=ALU.mult)
                ins.then_inc(scaled, 1)

            def add_residual(p, b):
                q = p - 1
                n = q * 2 + b + 1
                dve.wait_ge(rs1_done, n)
                dve.wait_ge(scaled, n)
                dve.wait_ge(xres_ready, q + 1)
                for c in range(NC):
                    ins = nc.vector.scalar_tensor_tensor(out=ln[:, b, c, :], in0=ln[:, b, c, :],
                                                         scalar=rs1[:, b, c:c + 1], in1=xres[:, b, c, :],
                                                         op0=ALU.mult, op1=ALU.add)
                ins.then_inc(ln1_done, 1)
                dve.wait_ge(ln1_done, n)
                for c in range(NC):
                    ins = nc.vector.bn_stats(bn2[:, b, c, :], ln[:, b, c, :])
                ins.then_inc(bn2_done, 1)
                reach_alone(dve, (s_setup, 1), (bn2_done, n))
                for c in range(NC):
                    ins = nc.vector.bn_aggr(mv2[:, b, c, :], bn2[:, b, c, :])
                ins.then_inc(mv2_done, 1)

            def second_norm(p, b):
                n = (p - 1) * 2 + b + 1
                dve.wait_ge(rs2_done, n)
                for c in range(NC):
                    ins = nc.vector.tensor_scalar(ln[:, b, c, :], ln[:, b, c, :], mv2[:, b, c, 0:1],
                                                  rs2[:, b, c:c + 1], ALU.subtract, ALU.mult)
                ins.then_inc(ln2_done, 1)

            one_now = [True]

            def step(p, one, two):
                one_now[0] = one
                if one:
                    copy_xt(p, 0), copy_xt(p, 1)
                    x_hi(p)
                if two:
                    v_lo_(p, 0, 0)
                if one:
                    factors(p, 0)
                if two:
                    v_lo_(p, 0, 1)
                if one:
                    logits(p, 0, 0), logits(p, 1, 0)
                    normalize(p, 0, 0)
                if two:
                    v_lo_(p, 1, 0)
                if one:
                    normalize(p, 1, 0)
                    logits(p, 0, 1)
                    normalize(p, 0, 1)
                if two:
                    v_lo_(p, 1, 1)
                if one:
                    pt_lo(p, 0, 0), pt_lo(p, 1, 0)
                    logits(p, 1, 1)
                    normalize(p, 1, 1)
                if two:
                    factors(p, 1)
                if one:
                    y_lo(p, 0, 0)
                    pt_lo(p, 0, 1)
                    y_lo(p, 1, 0)
                    pt_lo(p, 1, 1)
                if two:
                    logits(p, 0, H), logits(p, 1, H)
                    normalize(p, 0, H)
                if one:
                    y_lo(p, 0, 1)
                if two:
                    normalize(p, 1, H)
                if one:
                    elu(p, 0, 0)
                    y_lo(p, 1, 1)
                    logits(p, 0, 2)
                    elu(p, 0, 1)
                    logits(p, 1, 2)
                    normalize(p, 0, 2)
                if two:
                    pt_lo(p, 0, H), pt_lo(p, 1, H)
                if one:
                    normalize(p, 1, 2)
                if two:
                    elu_out(p, 0)
                if one:
                    elu(p, 1, 0)
                if two:
                    elu_out(p, 1)
                if one:
                    pt_lo(p, 0, 2), pt_lo(p, 1, 2)
                    elu(p, 1, 1)
                    y_lo(p, 0, 2), y_lo(p, 1, 2)
                    logits(p, 0, 3), logits(p, 1, 3)
                    normalize(p, 0, 3), normalize(p, 1, 3)
                if two:
                    ffn_hi(p, 0), ffn_hi(p, 1)
                if one:
                    elu(p, 2, 0)
                    pt_lo(p, 0, 3), pt_lo(p, 1, 3)
                    y_lo(p, 0, 3)
                    elu(p, 2, 1)
                    y_lo(p, 1, 3)
                    elu(p, 3, 0), elu(p, 3, 1)
                if two:
                    norm_stats(p, 0), norm_stats(p, 1)
                    add_residual(p, 0), add_residual(p, 1)
                    second_norm(p, 0), second_norm(p, 1)

            set_up()
            step(0, True, False)
            step(1, True, True)
            with dve.Fori(2, PAIRS) as p:
                step(p, True, True)
            step(PAIRS, False, True)


_INS = ['x', 'adj', 'L0_gnn_W_heads', 'L0_gnn_a_heads', 'L0_gnn_W_out', 'L0_gnn_a_out', 'L0_gnn_w1', 'L0_gnn_b1',
        'L0_gnn_w2', 'L0_gnn_b2', 'L0_gnn_ln_gamma', 'L0_gnn_ln_beta']
_OUTS = [((32, 256, 256), 'float32')]


def kernel(**inputs):
    import numpy as _np
    import concourse.bacc as _bacc
    from concourse import mybir as _mybir
    from concourse.bass_utils import run_bass_kernel_spmd as _run

    nc = _bacc.Bacc("TRN2", target_bir_lowering=False, num_devices=1)
    arrays, args = {}, []
    for name in _INS:
        a = _np.ascontiguousarray(inputs[name])
        arrays[f"in_{name}_dram"] = a
        args.append(nc.dram_tensor(f"in_{name}_dram", a.shape, _mybir.dt.from_np(a.dtype), kind="ExternalInput").ap())
    for i, (shape, dtype) in enumerate(_OUTS):
        dt = _mybir.dt.from_np(_np.dtype(dtype))
        args.append(nc.dram_tensor(f"out_{i}_dram", shape, dt, kind="ExternalOutput").ap())
    gat_block(nc, *args)
    r = _run(nc, [arrays], core_ids=[0])
    got = tuple(r.results[0][f"out_{i}_dram"] for i in range(len(_OUTS)))
    return got[0]
```

```python
from contextlib import ExitStack

import concourse.bass as bass
from concourse import mybir

F32 = mybir.dt.float32
F32R = mybir.dt.float32r
BF16 = mybir.dt.bfloat16
I32 = mybir.dt.int32
ACT = mybir.ActivationFunctionType
ALU = mybir.AluOpType
AX = mybir.AxisListType

P = 128
SLOPE = 0.01
MASKED = -1.0e9
EPS = 1e-5


def gat_block(nc: bass.Bass, x, adj, w_heads, a_heads, w_out, a_out, w1, b1, w2, b2, gamma, beta, out):
    B, N, F = x.shape
    H, _, O = w_heads.shape
    PAIRS = B // 2
    NC = N // P
    FC = F // P
    OC = O // P
    KC = H * OC
    FCOLS = 4
    W2N = O + FCOLS
    FROWS = 32
    assert N == F == O == 256 and H == 4 and w_out.shape == (H * O, O) and w1.shape == (O, O)

    ctx = ExitStack()
    with ctx:
        def sb(name, shape, dt):
            return ctx.enter_context(nc.sbuf_tensor(name, shape, dt))

        def sem(name):
            return ctx.enter_context(nc.semaphore(name))

        ident = sb("ident", [P, P], F32)
        ident_b = sb("ident_b", [P, P], BF16)
        ident_r = sb("ident_r", [P, P], F32R)
        ones_r = sb("ones_r", [P, P], F32R)
        mask = sb("mask", [P, NC, N], BF16)
        row_sel = sb("row_sel", [P, 3, 8], F32)
        row_w = sb("row_w", [P, 3], F32)
        wh = [sb(f"wh_{s}", [P, FC, H, O], F32R) for s in ("hi", "lo")]
        wo = [sb(f"wo_{s}", [P, KC, W2N], F32R) for s in ("hi", "lo")]
        w1s = [sb(f"w1_{s}", [P, OC, O], F32R) for s in ("hi", "lo")]
        w2s = [sb(f"w2_{s}", [P, OC, O], F32R) for s in ("hi", "lo")]
        u_in = [sb(f"u_in_{s}", [P, FC, FROWS], F32R) for s in ("hi", "lo")]
        u_out = sb("u_out", [P, KC, 2], F32)
        u_sum = sb("u_sum", [P, FC, 2 * H], F32)
        b1c = sb("b1c", [P, OC], F32)
        b2r = sb("b2r", [P, O], F32R)
        gamma_b = sb("gamma_b", [P, O], F32)
        beta_b = sb("beta_b", [P, O], F32)
        eps_c = sb("eps_c", [P, NC], F32)
        minus_half = sb("minus_half", [P, NC], F32)

        xn = sb("xn", [P, 2, NC, F], F32)
        xs = [sb(f"x_{s}", [P, 2, NC, F], F32R) for s in ("hi", "lo")]
        xt = [sb(f"xt_{s}", [P, FC, 2, N], F32R) for s in ("hi", "lo")]
        f_hi = sb("f_hi", [FROWS, 2 * N], F32R)
        f_sp = sb("f_sp", [FROWS, 2 * N], F32R)
        L = sb("L", [FROWS, H, 2 * N], F32R)
        R = sb("R", [FROWS, 2 * N], F32R)
        att = sb("att", [P, 3, 2, NC, N], F32)
        negmax = sb("negmax", [P, 3, 2, NC], F32)
        total = sb("total", [P, 3, 2, NC], F32)
        inv = sb("inv", [P, 3, 2, NC], F32)
        pt = [sb(f"pt_{s}", [P, 2, 2, NC, N], F32R) for s in ("hi", "lo")]
        yt = [sb(f"yt_{s}", [P, 2, FC, 2, N], F32R) for s in ("hi", "lo")]
        elu_w = sb("elu_w", [P, 4, 2 * N], F32)
        ht = [sb(f"ht_{s}", [P, KC, 2 * N], F32R) for s in ("hi", "lo")]
        v = [sb(f"v_{s}", [P, 2, NC, O], F32R) for s in ("hi", "lo")]
        f2pad = sb("f2pad", [P, 2, NC, P], F32)
        L2 = sb("L2", [FROWS, 2 * N], F32R)
        R2 = sb("R2", [FROWS, 2 * N], F32R)
        elu_o = sb("elu_o", [P, OC, 2 * N], F32)
        ot = [sb(f"ot_{s}", [P, OC, 2 * N], F32R) for s in ("hi", "lo")]
        rt = [sb(f"rt_{s}", [P, OC, 2 * N], F32R) for s in ("hi", "lo")]
        xres = sb("xres", [P, 2, NC, O], F32)
        ln = sb("ln", [P, 2, NC, O], F32)
        bn1 = sb("bn1", [P, 2, NC, 6], F32)
        mv1 = sb("mv1", [P, 2, NC, 2], F32)
        ve1 = sb("ve1", [P, 2, NC], F32)
        rs1 = sb("rs1", [P, 2, NC], F32)
        bn2 = sb("bn2", [P, 2, NC, 6], F32)
        mv2 = sb("mv2", [P, 2, NC, 2], F32)
        ve2 = sb("ve2", [P, 2, NC], F32)
        rs2 = sb("rs2", [P, 2, NC], F32)

        bank = [ctx.enter_context(nc.psum_tensor(f"bank{i}", [P, 512], F32)) for i in range(8)]
        PLAN = [(("xt", 0), 3), (("xt", 1), 5), (("v", 0, 0), 0), (("f",), 6), (("v", 0, 1), 5),
                (("z", 0, 0), 1), (("z", 1, 0), 7), (("z", 0, 1), 6), (("z", 1, 1), 5), (("v", 1, 0), 3),
                (("t", 0, 0), 7), (("z", 0, 2), 6), (("t", 1, 0), 2), (("v", 1, 1), 1), (("z", 1, 2), 7),
                (("t", 0, 1), 0), (("f2",), 5), (("y", 0, 0), 2), (("y", 1, 0), 6), (("z", 0, H), 4),
                (("z", 1, H), 5), (("t", 1, 1), 7), (("y", 0, 1), 3), (("z", 0, 3), 1), (("w", 0, 0), 4),
                (("w", 0, 1), 0), (("t", 0, H), 6), (("t", 0, 2), 5), (("t", 1, H), 2), (("y", 1, 1), 7),
                (("t", 1, 2), 6), (("o", 0), 2), (("o", 1), 4), (("y", 0, 2), 3), (("w", 1, 0), 1),
                (("z", 1, 3), 7), (("t", 0, 3), 5), (("y", 1, 2), 6), (("w", 1, 1), 3), (("g", 0), 4),
                (("g", 1), 0), (("y", 0, 3), 1), (("t", 1, 3), 2), (("w", 2, 0), 7), (("r", 0), 6),
                (("y", 1, 3), 5), (("r", 1), 4), (("w", 2, 1), 3), (("w", 3, 0), 2), (("w", 3, 1), 4)]
        TILES = [tile for tile, _ in PLAN]
        BANK = dict(PLAN)

        def second(tile):
            return tile[0] in ("v", "f2", "o", "g", "r") or (tile[0] in "zt" and tile[2] == H)

        def reach(eng, s, value):
            if not (isinstance(value, int) and value <= 0):
                eng.wait_ge(s, value)

        def reach_alone(eng, known, *counts):
            for s, n in counts:
                if not isinstance(n, int):
                    eng.compute_val(n)
            eng.wait_ge(*known)
            for s, n in counts:
                reach(eng, s, n)

        def att_slot(h):
            return {0: 0, 1: 1, H: 2, 2: 0, 3: 1}[h]

        def pt_slot(h):
            return {0: 0, 1: 1, H: 0, 2: 1, 3: 0}[h]

        wh_loaded, ah_loaded, adj_loaded, wo_loaded = (sem(f"{s}_loaded") for s in ("wh", "ah", "adj", "wo"))
        w12_loaded, b2_loaded, vectors_loaded = sem("w12_loaded"), sem("b2_loaded"), sem("vectors_loaded")
        consts_made, masks_made, u_made = sem("consts_made"), sem("masks_made"), sem("u_made")
        wh_hi_done, wh_split, wo_hi_done, wo_lo_done, out_made = (
            sem(s) for s in ("wh_hi_done", "wh_split", "wo_hi_done", "wo_lo_done", "out_made"))
        dve_chain, pool_chain = sem("dve_chain"), sem("pool_chain")
        x_loaded = sem("x_loaded")
        xt_ready, xt_hi_done, xt_split = sem("xt_ready"), sem("xt_hi_done"), sem("xt_split")
        x_hi_done, x_lo_done = sem("x_hi_done"), sem("x_lo_done")
        f_ready = [sem("f1_ready"), sem("f2_ready")]
        f_hi_done = [sem("f1_hi_done"), sem("f2_hi_done")]
        f_split = [sem("f1_split"), sem("f2_split")]
        lr_done = [sem("lr1_done"), sem("lr2_done")]
        z_ready = [sem("z1_ready"), sem("z2_ready")]
        relu_done = [sem("relu1_done"), sem("relu2_done")]
        logits_done = [sem("logits1_done"), sem("logits2_done")]
        exp_done = [sem("exp1_done"), sem("exp2_done")]
        inv_done = [sem("inv1_done"), sem("inv2_done")]
        probs_done = [sem("probs1_done"), sem("probs2_done")]
        t_ready = [sem("t1_ready"), sem("t2_ready")]
        pt_hi_done = [sem("pt1_hi_done"), sem("pt2_hi_done")]
        pt_lo_done = [sem("pt1_lo_done"), sem("pt2_lo_done")]
        y_ready, y_hi_done, y_lo_done = sem("y_ready"), sem("y_hi_done"), sem("y_lo_done")
        w_ready = sem("w_ready")
        w_exp, w_neg, w_elu, w_hi, w_lo = (sem(f"w_{s}") for s in ("exp", "neg", "elu", "hi", "lo"))
        v_ready, v_hi, v_lo, f2_cols = (sem(s) for s in ("v_ready", "v_hi_done", "v_lo_done", "f2_cols"))
        o_ready = sem("o_ready")
        o_exp, o_neg, o_elu, o_hi, o_lo = (sem(f"o_{s}") for s in ("exp", "neg", "elu", "hi", "lo"))
        g_ready, g_hi, g_lo = (sem(f"g_{s}") for s in ("ready", "hi", "lo"))
        r_ready = sem("r_ready")
        xres_loaded, xres_ready = sem("xres_loaded"), sem("xres_ready")
        bn1_done, mv1_done, ve1_done, rs1_done = (sem(s) for s in ("bn1_done", "mv1_done", "ve1_done", "rs1_done"))
        scaled, ln1_done = sem("scaled"), sem("ln1_done")
        bn2_done, mv2_done, ve2_done, rs2_done = (sem(s) for s in ("bn2_done", "mv2_done", "ve2_done", "rs2_done"))
        ln2_done = sem("ln2_done")
        stored = sem("stored")

        def item(layer, pair, b, h):
            return pair * (2 * H) + 2 * h + b + 1 if layer == 0 else pair * 2 + b + 1

        def layer_of(h):
            return 1 if h == H else 0

        def read_out(tile, p):
            kind, at = tile[0], tile[1:]
            q = p - 1
            if kind in "zt":
                ly = layer_of(at[1])
                return (logits_done if kind == "z" else pt_lo_done)[ly], item(ly, p - ly, *at)
            if kind == "xt":
                return xt_split, p * 2 + at[0] + 1
            if kind == "f":
                return f_split[0], p + 1
            if kind == "f2":
                return f_split[1], q + 1
            if kind == "y":
                return y_lo_done, item(0, p, *at)
            if kind == "w":
                return w_elu, p * KC + OC * at[0] + at[1] + 1
            if kind == "v":
                return v_lo, q * 4 + 2 * at[0] + at[1] + 1
            return {"o": o_elu, "g": g_hi, "r": scaled}[kind], q * 2 + at[0] + 1

        x_rows = x.rearrange("b (c n) f -> n (b c) f", n=P)
        out_rows = out.rearrange("b (c n) f -> n (b c) f", n=P)

        raw_wh = [t[:, :, :, :].rearrange("p b c o -> p (b c o)") for t in (xres, ln)]
        raw_w12 = raw_wh[0]
        raw_ao = raw_wh[1][:, 0:2 * O]
        raw_ah = att[:, 0:2, :, :, :].rearrange("p s b c m -> p (s b c m)")
        raw_wo = [att[:, 2, :, :, :].rearrange("p b c m -> p (b c m)"), elu_o[:, :, :].rearrange("p c n -> p (c n)")]
        raw_adj, raw_b2, b2_hi = elu_w[:, 0, :].bitcast(I32), elu_w[0:2, 1, 0:O], elu_w[0:2, 1, O:2 * O].bitcast(F32R)
        junk_in = [elu_w[:, 2 + i // 2, (i % 2) * O:(i % 2 + 1) * O] for i in range(4)]
        junk_out = [raw_wh[1][:, (2 + i) * O:(3 + i) * O] for i in range(2)]

        block = ctx.enter_context(nc.Block())

        @block.sync
        def _(sp):
            sp.dma_start(xn[:, :, :, :].rearrange("p b c f -> p (b c) f"), x_rows[:, 0:2 * NC, :]).then_inc(x_loaded, 16)
            for c in range(FC):
                sp.dma_start(raw_wh[c].rearrange("p (h o) -> p h o", h=H),
                             w_heads[:, c * P:(c + 1) * P, :].rearrange("h f o -> f h o")).then_inc(wh_loaded, 16)
            sp.dma_start(raw_wo[0].rearrange("p (k o) -> p k o", o=O),
                         w_out[0:KC * P // 2, :].rearrange("(k p) o -> p k o", p=P)).then_inc(wo_loaded, 16)
            sp.dma_start(raw_wo[1].rearrange("p (k o) -> p k o", o=O),
                         w_out[KC * P // 2:KC * P, :].rearrange("(k p) o -> p k o", p=P)).then_inc(wo_loaded, 16)

            def load_next(p):
                reach_alone(sp, (x_loaded, 16), (xt_ready, p * 2 + 2), (x_hi_done, p + 1), (x_lo_done, p + 1))
                sp.dma_start(xn[:, :, :, :].rearrange("p b c f -> p (b c) f"),
                             x_rows[:, bass.ds(p * (2 * NC) + 2 * NC, 2 * NC), :]).then_inc(x_loaded, 16)

            def load_residual(q):
                reach_alone(sp, (x_loaded, 16), (ln1_done, q * 2))
                sp.dma_start(xres[:, :, :, :].rearrange("p b c f -> p (b c) f"),
                             x_rows[:, bass.ds(q * (2 * NC), 2 * NC), :]).then_inc(xres_loaded, 16)

            def store(q):
                for b in range(2):
                    reach_alone(sp, (x_loaded, 16), (ln2_done, q * 2 + b + 1))
                    sp.dma_start(out_rows[:, bass.ds(q * (2 * NC) + b * NC, NC), :], ln[:, b, :, :]).then_inc(stored, 16)

            load_next(0)
            sp.wait_ge(wh_split, 1)
            for i, w in enumerate((w1, w2)):
                sp.dma_start(raw_w12[:, i * OC * O:(i + 1) * OC * O].rearrange("p (c o) -> p c o", c=OC),
                             w.rearrange("(c p) o -> p c o", p=P)).then_inc(w12_loaded, 16)
            sp.dma_start(raw_ao, a_out.partition_broadcast(P)).then_inc(vectors_loaded, 16)
            sp.wait_ge(out_made, 1)
            load_residual(0)
            load_next(1)
            store(0)
            with sp.Fori(2, PAIRS - 1) as p:
                load_residual(p - 1)
                load_next(p)
                store(p - 1)
            for p in (PAIRS - 1, PAIRS):
                load_residual(p - 1)
                store(p - 1)
            sp.wait_ge(stored, PAIRS * 32)

        @block.gpsimd
        def _(pool):
            def link(ins, n):
                ins.then_inc(pool_chain, 1)
                pool.wait_ge(pool_chain, n)

            link(nc.gpsimd.memset(ident[:, :], 0.0), 1)
            link(nc.gpsimd.affine_select(out=ident[:, :], in_=ident[:, :], compare_op=ALU.not_equal, fill=1.0,
                                         base=0, pattern=[[-1, P]], channel_multiplier=1), 2)
            link(nc.gpsimd.memset(row_sel[:, :, :], 0.0), 3)
            n = 3
            for kind, off in ((0, 0), (0, 1), (1, 2), (1, 3)):
                n += 1
                sel = row_sel[:, kind, 0:H]
                link(nc.gpsimd.affine_select(out=sel, in_=sel, compare_op=ALU.not_equal, fill=1.0,
                                             base=-off, pattern=[[-4, H]], channel_multiplier=1), n)
            sel = row_sel[:, 2, :]
            link(nc.gpsimd.affine_select(out=sel, in_=sel, compare_op=ALU.not_equal, fill=-1.0,
                                         base=-1, pattern=[[-2, 2 * H]], channel_multiplier=1), n + 1)
            nc.gpsimd.memset(eps_c[:, :], EPS)
            nc.gpsimd.memset(minus_half[:, :], -0.5).then_inc(consts_made, 1)

            def x_lo(p):
                pool.wait_ge(x_hi_done, p + 1)
                nc.gpsimd.tensor_tensor(xs[1][:, :, :, :], xn[:, :, :, :], xs[0][:, :, :, :],
                                        ALU.subtract).then_inc(x_lo_done, 1)

            def h_lo(p, h, oc):
                pool.wait_ge(w_hi, p * KC + OC * h + oc + 1)
                s = (OC * h + oc) % 4
                nc.gpsimd.tensor_tensor(ht[1][:, OC * h + oc, :], elu_w[:, s, :], ht[0][:, OC * h + oc, :],
                                        ALU.subtract).then_inc(w_lo, 1)

            def split_w_out():
                pool.wait_ge(wo_hi_done, 1)
                for j in range(2):
                    nc.gpsimd.tensor_tensor(wo[1][:, 4 * j:4 * j + 4, 0:O],
                                            raw_wo[j].rearrange("p (k o) -> p k o", o=O),
                                            wo[0][:, 4 * j:4 * j + 4, 0:O], ALU.subtract).then_inc(wo_lo_done, 1)

            def residual(q):
                pool.wait_ge(xres_loaded, q * 16 + 16)
                nc.gpsimd.tensor_tensor(xres[:, :, :, :].rearrange("p b c o -> p (b c) o"),
                                        xres[:, :, :, :].rearrange("p b c o -> p (b c) o"),
                                        beta_b[:, :].unsqueeze(1).broadcast_to([P, 2 * NC, O]),
                                        ALU.add).then_inc(xres_ready, 1)

            def o_lo_(q, oc):
                pool.wait_ge(o_hi, q * 2 + oc + 1)
                nc.gpsimd.tensor_tensor(ot[1][:, oc, :], elu_o[:, oc, :], ot[0][:, oc, :],
                                        ALU.subtract).then_inc(o_lo, 1)

            def r_lo_(q, dc):
                pool.wait_ge(g_hi, q * 2 + dc + 1)
                nc.gpsimd.tensor_tensor(rt[1][:, dc, :], elu_o[:, dc, :], rt[0][:, dc, :],
                                        ALU.subtract).then_inc(g_lo, 1)

            def rstd(q, b, mv, ve, rs, mv_done, ve_done, rs_done):
                pool.wait_ge(mv_done, q * 2 + b + 1)
                nc.gpsimd.tensor_tensor(ve[:, b, :], mv[:, b, :, 1], eps_c[:, :], ALU.add).then_inc(ve_done, 1)
                pool.wait_ge(ve_done, q * 2 + b + 1)
                nc.gpsimd.tensor_tensor(rs[:, b, :], ve[:, b, :], minus_half[:, :], ALU.pow).then_inc(rs_done, 1)

            def rstd1(q, b):
                rstd(q, b, mv1, ve1, rs1, mv1_done, ve1_done, rs1_done)

            def rstd2(q, b):
                rstd(q, b, mv2, ve2, rs2, mv2_done, ve2_done, rs2_done)

            def step(p, one, two):
                q = p - 1
                first = isinstance(p, int) and p == 0
                if two:
                    residual(q)
                if one:
                    x_lo(p)
                    if first:
                        split_w_out()
                if two:
                    o_lo_(q, 0), o_lo_(q, 1)
                if one:
                    h_lo(p, 0, 0)
                if two:
                    r_lo_(q, 0), r_lo_(q, 1)
                if one:
                    h_lo(p, 0, 1)
                if two:
                    rstd1(q, 0)
                if one:
                    h_lo(p, 1, 0), h_lo(p, 1, 1), h_lo(p, 2, 0)
                if two:
                    rstd1(q, 1), rstd2(q, 0)
                if one:
                    h_lo(p, 2, 1), h_lo(p, 3, 0)
                if two:
                    rstd2(q, 1)
                if one:
                    h_lo(p, 3, 1)

            step(0, True, False)
            step(1, True, True)
            with pool.Fori(2, PAIRS) as p:
                step(p, True, True)
            step(PAIRS, False, True)

        @block.tensor
        def _(pe):
            held, order = {}, []

            def take(tile, p):
                b = BANK[tile]
                if b in held:
                    pe.wait_ge(*read_out(held[b], p))
                elif not (isinstance(p, int) and p == 0):
                    there = [t for t in TILES if BANK[t] == b]
                    for layer in (1, 2):
                        last = [t for t in there if second(t) == (layer == 2)][-1:]
                        if last:
                            reach(pe, *read_out(last[0], p - 1))
                held[b] = tile
                order.append(tile)
                return bank[b]

            def split_product(ps, lhs, rhs, n, start=True, last_stop=True):
                for i in range(n):
                    for j, (a, b) in enumerate(((0, 0), (1, 0), (0, 1))):
                        mm = nc.tensor.matmul(ps, lhs(a, i), rhs(b, i), start=(start and i == 0 and j == 0),
                                              stop=(last_stop and i == n - 1 and j == 2))
                return mm

            def transpose_x(p, b):
                ps = take(("xt", b), p)
                if b == 0:
                    pe.wait_ge(x_loaded, p * 16 + 16)
                for fc in range(FC):
                    for c in range(NC):
                        mm = nc.tensor.transpose(ps[:, fc * N + c * P:fc * N + (c + 1) * P],
                                                 xn[:, b, c, fc * P:(fc + 1) * P], ident[:, :])
                mm.then_inc(xt_ready, 1)

            def f_rows(p):
                ps = take(("f",), p)
                if isinstance(p, int) and p == 0:
                    pe.wait_ge(u_made, 1)
                pe.wait_ge(xt_split, p * 2 + 2)
                split_product(ps[0:FROWS, :], lambda s, i: u_in[s][:, i, :],
                              lambda s, i: xt[s][:, i, :, :].rearrange("p b n -> p (b n)"), FC).then_inc(f_ready[0], 1)

            def f2_rows(p):
                ps = take(("f2",), p)
                pe.wait_ge(f2_cols, (p - 1) * 4 + 4)
                for b in range(2):
                    for c in range(NC):
                        mm = nc.tensor.transpose(ps[:, b * N + c * P:b * N + (c + 1) * P], f2pad[:, b, c, :], ident[:, :])
                mm.then_inc(f_ready[1], 1)

            def scores(p, b, h):
                ps = take(("z", b, h), p)
                ly = layer_of(h)
                pe.wait_ge(lr_done[ly], p - ly + 1)
                lhs, rhs = (L[:, h, :], R) if ly == 0 else (L2, R2)
                if isinstance(p, int) and p == 0 and (b, h) == (0, 0):
                    pe.wait_ge(masks_made, 1)
                for c in range(NC):
                    region = ps[:, c * N:(c + 1) * N]
                    nc.tensor.matmul(region, ident_b[:, :], mask[:, c, :], start=True, stop=False)
                    mm = nc.tensor.matmul(region, lhs[:, b * N + c * P:b * N + (c + 1) * P], rhs[:, b * N:(b + 1) * N],
                                          start=False, stop=True)
                mm.then_inc(z_ready[ly], 1)

            def transpose_probs(p, b, h):
                ps = take(("t", b, h), p)
                ly = layer_of(h)
                pe.wait_ge(probs_done[ly], item(ly, p - ly, b, h))
                for mc in range(NC):
                    for c in range(NC):
                        mm = nc.tensor.transpose(ps[:, mc * N + c * P:mc * N + (c + 1) * P],
                                                 att[:, att_slot(h), b, c, mc * P:(mc + 1) * P], ident[:, :])
                mm.then_inc(t_ready[ly], 1)

            def attend_x(p, b, h):
                ps = take(("y", b, h), p)
                pe.wait_ge(pt_hi_done[0], item(0, p, b, h))
                pe.wait_ge(pt_lo_done[0], item(0, p, b, h))
                if h == 0 and b == 0:
                    pe.wait_ge(x_lo_done, p + 1)
                for fc in range(FC):
                    mm = split_product(ps[:, fc * N:(fc + 1) * N],
                                       lambda s, i: xs[s][:, b, i, fc * P:(fc + 1) * P],
                                       lambda s, i: pt[s][:, pt_slot(h), b, i, :], NC)
                mm.then_inc(y_ready, 1)

            def project_head(p, h, oc):
                ps = take(("w", h, oc), p)
                if isinstance(p, int) and p == 0 and (h, oc) == (0, 0):
                    pe.wait_ge(wh_split, 1)
                pe.wait_ge(y_hi_done, item(0, p, 1, h))
                pe.wait_ge(y_lo_done, item(0, p, 1, h))
                split_product(ps[:, :], lambda s, i: wh[s][:, i, h, oc * P:(oc + 1) * P],
                              lambda s, i: yt[s][:, h % 2, i, :, :].rearrange("p b n -> p (b n)"),
                              FC).then_inc(w_ready, 1)

            def project_out(p, b, mc):
                ps = take(("v", b, mc), p)
                for k in range(KC):
                    pe.wait_ge(w_lo, (p - 1) * KC + k + 1)
                    for j, (s, t) in enumerate(((0, 0), (1, 0), (0, 1))):
                        mm = nc.tensor.matmul(ps[:, 0:W2N], ht[s][:, k, b * N + mc * P:b * N + (mc + 1) * P],
                                              wo[t][:, k, :], start=(k == 0 and j == 0), stop=(k == KC - 1 and j == 2))
                mm.then_inc(v_ready, 1)

            def attend_out(p, oc):
                ps = take(("o", oc), p)
                q = p - 1
                pe.wait_ge(v_lo, q * 4 + 4)
                for b in range(2):
                    pe.wait_ge(pt_hi_done[1], item(1, q, b, H))
                    pe.wait_ge(pt_lo_done[1], item(1, q, b, H))
                    mm = split_product(ps[:, b * N:(b + 1) * N],
                                       lambda s, i: v[s][:, b, i, oc * P:(oc + 1) * P],
                                       lambda s, i: pt[s][:, pt_slot(H), b, i, :], NC)
                mm.then_inc(o_ready, 1)

            def ffn_in(p, dc):
                ps = take(("g", dc), p)
                pe.wait_ge(o_lo, (p - 1) * 2 + 2)
                split_product(ps[:, :], lambda s, i: w1s[s][:, i, dc * P:(dc + 1) * P],
                              lambda s, i: ot[s][:, i, :], OC).then_inc(g_ready, 1)

            def ffn_out(p, b):
                ps = take(("r", b), p)
                pe.wait_ge(g_lo, (p - 1) * 2 + 2)
                for c in range(NC):
                    cols = slice(b * N + c * P, b * N + (c + 1) * P)
                    nc.tensor.matmul(ps[:, c * O:(c + 1) * O], ones_r[:, :], b2r[:, :], start=True, stop=False)
                    split_product(ps[:, c * O:(c + 1) * O], lambda s, i: rt[s][:, i, cols],
                                  lambda s, i: w2s[s][:, i, :], OC, start=False, last_stop=False)
                    for oc in range(OC):
                        for s in range(2):
                            mm = nc.tensor.matmul(ps[:, c * O + oc * P:c * O + (oc + 1) * P], ot[s][:, oc, cols],
                                                  ident_r[:, :], start=False, stop=(oc == OC - 1 and s == 1))
                mm.then_inc(r_ready, 1)

            def step(p, one, two):
                held.clear()
                order.clear()
                if one:
                    transpose_x(p, 0), transpose_x(p, 1)
                if two:
                    project_out(p, 0, 0)
                if one:
                    f_rows(p)
                if two:
                    project_out(p, 0, 1)
                if one:
                    scores(p, 0, 0), scores(p, 1, 0), scores(p, 0, 1), scores(p, 1, 1)
                if two:
                    project_out(p, 1, 0)
                if one:
                    transpose_probs(p, 0, 0), scores(p, 0, 2), transpose_probs(p, 1, 0)
                if two:
                    project_out(p, 1, 1)
                if one:
                    scores(p, 1, 2), transpose_probs(p, 0, 1)
                if two:
                    f2_rows(p)
                if one:
                    attend_x(p, 0, 0), attend_x(p, 1, 0)
                if two:
                    scores(p, 0, H), scores(p, 1, H)
                if one:
                    transpose_probs(p, 1, 1), attend_x(p, 0, 1), scores(p, 0, 3), project_head(p, 0, 0)
                    project_head(p, 0, 1)
                if two:
                    transpose_probs(p, 0, H)
                if one:
                    transpose_probs(p, 0, 2)
                if two:
                    transpose_probs(p, 1, H)
                if one:
                    attend_x(p, 1, 1), transpose_probs(p, 1, 2)
                if two:
                    attend_out(p, 0), attend_out(p, 1)
                if one:
                    attend_x(p, 0, 2), project_head(p, 1, 0), scores(p, 1, 3), transpose_probs(p, 0, 3)
                    attend_x(p, 1, 2), project_head(p, 1, 1)
                if two:
                    ffn_in(p, 0), ffn_in(p, 1)
                if one:
                    attend_x(p, 0, 3), transpose_probs(p, 1, 3), project_head(p, 2, 0)
                if two:
                    ffn_out(p, 0)
                if one:
                    attend_x(p, 1, 3)
                if two:
                    ffn_out(p, 1)
                if one:
                    project_head(p, 2, 1), project_head(p, 3, 0), project_head(p, 3, 1)

            pe.wait_ge(consts_made, 1)
            step(0, True, False)
            pe.wait_ge(out_made, 1)
            step(1, True, True)
            with pe.Fori(2, PAIRS) as p:
                step(p, True, True)
            assert order == TILES
            step(PAIRS, False, True)

        @block.scalar
        def _(act):
            def split_f(p, ly):
                ps = bank[BANK[("f",) if ly == 0 else ("f2",)]]
                act.wait_ge(f_ready[ly], p - ly + 1)
                rows = FROWS if ly == 0 else 4
                if ly == 0:
                    reach(act, f_split[1], p - 1)
                    reach(act, f_split[0], p)
                else:
                    act.wait_ge(f_split[0], p + 1 if one_now[0] else PAIRS)
                nc.scalar.activation(f_hi[0:rows, :], ps[0:rows, :], ACT.Copy).then_inc(f_hi_done[ly], 1)

            def relu_part(p, b, h):
                ly = layer_of(h)
                n = item(ly, p - ly, b, h)
                act.wait_ge(z_ready[ly], n)
                if h == H:
                    reach(act, t_ready[1], (p - 1) * 2)
                else:
                    reach(act, t_ready[0], item(0, p - 1, b, h + 2) if h < 2 else item(0, p, b, h - 2))
                nc.scalar.activation(att[:, att_slot(h), b, :, :].rearrange("p c m -> p (c m)"),
                                     bank[BANK[("z", b, h)]][:, :], ACT.Relu,
                                     scale=(1.0 - SLOPE) / SLOPE).then_inc(relu_done[ly], 1)

            def exps(p, b, h):
                ly, s = layer_of(h), att_slot(h)
                n = item(ly, p - ly, b, h)
                act.wait_ge(logits_done[ly], n)
                for c in range(NC):
                    ins = nc.scalar.activation(att[:, s, b, c, :], att[:, s, b, c, :], ACT.Exp, scale=-1.0,
                                               bias=negmax[:, s, b, c:c + 1], accum_out=total[:, s, b, c:c + 1])
                ins.then_inc(exp_done[ly], 1)

            def pt_hi(p, b, h):
                ly = layer_of(h)
                act.wait_ge(t_ready[ly], item(ly, p - ly, b, h))
                if h in (0, 2):
                    reach(act, y_ready, item(0, p - 1, b, 3) if h == 0 else item(0, p, b, 1))
                elif h == 1:
                    reach(act, y_ready, item(0, p - 1, b, 2))
                elif h == H:
                    reach(act, y_ready, item(0, p, b, 0) if one_now[0] else PAIRS * 2 * H)
                elif two_now[0]:
                    act.wait_ge(o_ready, (p - 1) * 2 + 2)
                else:
                    act.wait_ge(y_ready, item(0, p, b, 0))
                nc.scalar.activation(pt[0][:, pt_slot(h), b, :, :].rearrange("p c n -> p (c n)"),
                                     bank[BANK[("t", b, h)]][:, :], ACT.Copy).then_inc(pt_hi_done[ly], 1)

            def y_hi(p, b, h):
                act.wait_ge(y_ready, item(0, p, b, h))
                reach(act, w_ready, p * KC + OC * (h - 1) if h >= 2 else p * KC - KC + OC * (h + 3))
                nc.scalar.activation(yt[0][:, h % 2, :, b, :], bank[BANK[("y", b, h)]][:, :].rearrange(
                    "p (c n) -> p c n", c=FC), ACT.Copy).then_inc(y_hi_done, 1)

            def copy_xt(p, b):
                act.wait_ge(xt_ready, p * 2 + b + 1)
                reach(act, f_ready[0], p)
                nc.scalar.activation(xt[0][:, :, b, :], bank[BANK[("xt", b)]][:, :].rearrange(
                    "p (c n) -> p c n", c=FC), ACT.Copy).then_inc(xt_hi_done, 1)

            def w_exp_(p, h, oc):
                i = OC * h + oc
                act.wait_ge(w_ready, p * KC + i + 1)
                reach(act, w_lo, p * KC + i + 1 - 4)
                nc.scalar.activation(elu_w[:, i % 4, :], bank[BANK[("w", h, oc)]][:, :], ACT.Exp).then_inc(w_exp, 1)

            def w_neg_(p, h, oc):
                i = OC * h + oc
                act.wait_ge(w_exp, p * KC + i + 1)
                nc.scalar.activation(elu_w[:, i % 4, :], elu_w[:, i % 4, :], ACT.Relu, scale=-1.0,
                                     bias=1.0).then_inc(w_neg, 1)

            def h_hi(p, h, oc):
                i = OC * h + oc
                act.wait_ge(w_elu, p * KC + i + 1)
                if i == 0:
                    reach(act, v_ready, p * 4)
                nc.scalar.activation(ht[0][:, i, :], elu_w[:, i % 4, :], ACT.Copy).then_inc(w_hi, 1)

            def v_hi_(p, b, mc):
                q = p - 1
                i = 2 * b + mc
                act.wait_ge(v_ready, q * 4 + i + 1)
                reach(act, o_ready, q * 2)
                reach(act, f_ready[1], q)
                ps = bank[BANK[("v", b, mc)]]
                nc.scalar.activation(v[0][:, b, mc, :], ps[:, 0:O], ACT.Copy).then_inc(v_hi, 1)
                nc.scalar.activation(f2pad[:, b, mc, 0:FCOLS], ps[:, O:W2N], ACT.Copy).then_inc(f2_cols, 1)

            def o_exp_(p, oc):
                q = p - 1
                act.wait_ge(o_ready, q * 2 + oc + 1)
                reach(act, g_lo, q * 2)
                nc.scalar.activation(elu_o[:, oc, :], bank[BANK[("o", oc)]][:, :], ACT.Exp).then_inc(o_exp, 1)

            def o_neg_(p, oc):
                q = p - 1
                act.wait_ge(o_exp, q * 2 + oc + 1)
                nc.scalar.activation(elu_o[:, oc, :], elu_o[:, oc, :], ACT.Relu, scale=-1.0, bias=1.0).then_inc(o_neg, 1)

            def o_hi_(p, oc):
                q = p - 1
                act.wait_ge(o_elu, q * 2 + oc + 1)
                reach(act, r_ready, q * 2)
                nc.scalar.activation(ot[0][:, oc, :], elu_o[:, oc, :], ACT.Copy).then_inc(o_hi, 1)

            def ffn_relu(p, dc):
                q = p - 1
                act.wait_ge(g_ready, q * 2 + dc + 1)
                nc.scalar.activation(elu_o[:, dc, :], bank[BANK[("g", dc)]][:, :], ACT.Relu, bias=b1c[:, dc:dc + 1])

            def ffn_relu_hi(p, dc):
                nc.scalar.activation(rt[0][:, dc, :], bank[BANK[("g", dc)]][:, :], ACT.Relu,
                                     bias=b1c[:, dc:dc + 1]).then_inc(g_hi, 1)

            def w_out_hi():
                act.wait_ge(wo_loaded, 32)
                for j in range(2):
                    ins = nc.scalar.activation(wo[0][:, 4 * j:4 * j + 4, 0:O],
                                               raw_wo[j].rearrange("p (k o) -> p k o", o=O), ACT.Copy)
                ins.then_inc(wo_hi_done, 1)

            one_now, two_now = [True], [True]

            def step(p, one, two):
                one_now[0], two_now[0] = one, two
                first = isinstance(p, int) and p == 0
                if one:
                    copy_xt(p, 0), copy_xt(p, 1)
                if two:
                    v_hi_(p, 0, 0)
                if one:
                    split_f(p, 0)
                if two:
                    v_hi_(p, 0, 1)
                if one:
                    relu_part(p, 0, 0), relu_part(p, 1, 0), relu_part(p, 0, 1), exps(p, 0, 0), exps(p, 1, 0)
                    relu_part(p, 1, 1), exps(p, 0, 1), relu_part(p, 0, 2), pt_hi(p, 0, 0), exps(p, 1, 1)
                if two:
                    v_hi_(p, 1, 0)
                if one:
                    pt_hi(p, 1, 0)
                if two:
                    v_hi_(p, 1, 1)
                if one:
                    relu_part(p, 1, 2), pt_hi(p, 0, 1)
                if two:
                    split_f(p, 1)
                if one:
                    exps(p, 0, 2), y_hi(p, 0, 0), exps(p, 1, 2)
                if two:
                    relu_part(p, 0, H)
                if one:
                    y_hi(p, 1, 0)
                    if first:
                        w_out_hi()
                    pt_hi(p, 1, 1)
                if two:
                    relu_part(p, 1, H), exps(p, 0, H)
                if one:
                    relu_part(p, 0, 3)
                if two:
                    exps(p, 1, H)
                if one:
                    w_exp_(p, 0, 0), w_exp_(p, 0, 1)
                if two:
                    pt_hi(p, 0, H)
                if one:
                    pt_hi(p, 0, 2)
                if two:
                    pt_hi(p, 1, H)
                if one:
                    w_neg_(p, 0, 0), y_hi(p, 0, 1), y_hi(p, 1, 1), pt_hi(p, 1, 2), exps(p, 0, 3)
                if two:
                    o_exp_(p, 0), o_neg_(p, 0), o_exp_(p, 1), o_neg_(p, 1)
                if one:
                    y_hi(p, 0, 2)
                if two:
                    o_hi_(p, 0)
                if one:
                    w_neg_(p, 0, 1), w_exp_(p, 1, 0)
                if two:
                    o_hi_(p, 1)
                if one:
                    w_neg_(p, 1, 0), relu_part(p, 1, 3), h_hi(p, 0, 0), pt_hi(p, 0, 3), exps(p, 1, 3)
                    y_hi(p, 1, 2)
                if two:
                    ffn_relu(p, 0), ffn_relu_hi(p, 0), ffn_relu(p, 1), ffn_relu_hi(p, 1)
                if one:
                    w_exp_(p, 1, 1), w_neg_(p, 1, 1), y_hi(p, 0, 3), pt_hi(p, 1, 3), w_exp_(p, 2, 0)
                    w_neg_(p, 2, 0), h_hi(p, 0, 1), y_hi(p, 1, 3), h_hi(p, 1, 0), h_hi(p, 1, 1)
                    h_hi(p, 2, 0), w_exp_(p, 2, 1), w_neg_(p, 2, 1), w_exp_(p, 3, 0), w_neg_(p, 3, 0)
                    h_hi(p, 2, 1), w_exp_(p, 3, 1), h_hi(p, 3, 0), w_neg_(p, 3, 1), h_hi(p, 3, 1)

            act.dma_start(raw_ah, a_heads.rearrange("h c -> (h c)").partition_broadcast(P)).then_inc(ah_loaded, 16)
            act.dma_start(raw_adj.rearrange("p (c m) -> p c m", c=NC),
                          adj.rearrange("(c n) m -> n c m", n=P)).then_inc(adj_loaded, 16)
            act.dma_start(raw_b2, b2.partition_broadcast(2)).then_inc(b2_loaded, 16)
            act.dma_start(b1c[:, :], b1.rearrange("(c p) -> p c", p=P), allow_slow_non_contiguous=True).then_inc(vectors_loaded, 16)
            act.dma_start(gamma_b[:, :], gamma.partition_broadcast(P)).then_inc(vectors_loaded, 16)
            act.dma_start(beta_b[:, :], beta.partition_broadcast(P)).then_inc(vectors_loaded, 16)
            act.wait_ge(wh_loaded, 16 * FC)
            for c in range(FC):
                ins = nc.scalar.activation(wh[0][:, c, :, :].rearrange("p h o -> p (h o)"), raw_wh[c], ACT.Copy)
            ins.then_inc(wh_hi_done, 1)
            step(0, True, False)
            step(1, True, True)
            with act.Fori(2, PAIRS) as p:
                step(p, True, True)
            step(PAIRS, False, True)

        @block.vector
        def _(dve):
            chain = [0]

            def link(ins):
                chain[0] += 1
                ins.then_inc(dve_chain, 1)
                dve.wait_ge(dve_chain, chain[0])

            def set_up():
                for t in (L2, R2, b2r):
                    nc.vector.memset(t[:, :].bitcast(F32), 0.0)
                nc.vector.memset(ones_r[:, :].bitcast(F32), 1.0)
                nc.vector.memset(f2pad[:, :, :, :], 0.0)
                for t in u_in:
                    link(nc.vector.memset(t[:, :, :].bitcast(F32), 0.0))
                dve.wait_ge(consts_made, 1)
                nc.vector.tensor_copy(ident_b[:, :], ident[:, :])
                nc.vector.tensor_copy(ident_r[:, :], ident[:, :])
                link(nc.vector.tensor_reduce(row_w[:, :], row_sel[:, :, :], AX.X, ALU.add))
                dve.wait_ge(adj_loaded, 16)
                nc.vector.tensor_scalar(mask[:, :, :].rearrange("p c m -> p (c m)"), raw_adj, 0.0, MASKED,
                                        ALU.is_le, ALU.mult).then_inc(masks_made, 1)
                dve.wait_ge(b2_loaded, 16)
                link(nc.vector.tensor_copy(b2_hi, raw_b2))
                nc.vector.scalar_tensor_tensor(out=b2r[0:2, :], in0=b2_hi, scalar=row_w[0:2, 2:3],
                                               in1=raw_b2, op0=ALU.mult, op1=ALU.add)
                dve.wait_ge(ah_loaded, 16)
                for c in range(FC):
                    dve.wait_ge(wh_loaded, 16 * FC)
                    for i in range(2 * H):
                        ins = nc.vector.tensor_tensor_reduce(
                            junk_in[i % 4], raw_wh[c][:, (i // 2) * O:(i // 2 + 1) * O], raw_ah[:, i * O:(i + 1) * O],
                            SLOPE, 0.0, ALU.mult, ALU.add, u_sum[:, c, i:i + 1])
                        if i % 4 == 3:
                            link(ins)
                hi, lo = (t[:, :, 0:4 * H].rearrange("p c (i e) -> p c i e", e=2) for t in u_in)
                for e in range(2):
                    ins = nc.vector.tensor_copy(hi[:, :, :, e], u_sum[:, :, :])
                link(ins)
                for e in range(2):
                    ins = nc.vector.tensor_tensor(lo[:, :, :, e], u_sum[:, :, :], hi[:, :, :, e], ALU.subtract)
                ins.then_inc(u_made, 1)

            def split_w_heads():
                dve.wait_ge(wh_hi_done, 1)
                for c in range(FC):
                    ins = nc.vector.tensor_tensor(wh[1][:, c, :, :].rearrange("p h o -> p (h o)"), raw_wh[c],
                                                  wh[0][:, c, :, :].rearrange("p h o -> p (h o)"), ALU.subtract)
                ins.then_inc(wh_split, 1)

            def out_columns(j):
                dve.wait_ge(vectors_loaded, 16 * 4)
                dve.wait_ge(wo_loaded, 32)
                for k in range(4):
                    for i in range(2):
                        ins = nc.vector.tensor_tensor_reduce(junk_out[i], raw_wo[j][:, k * O:(k + 1) * O],
                                                             raw_ao[:, i * O:(i + 1) * O], SLOPE, 0.0, ALU.mult,
                                                             ALU.add, u_out[:, 4 * j + k, i:i + 1])
                    link(ins)

            def split_ffn():
                dve.wait_ge(w12_loaded, 32)
                parts = [[t[:, :, :].rearrange("p c o -> p (c o)") for t in w] for w in (w1s, w2s)]
                raws = [raw_w12[:, i * OC * O:(i + 1) * OC * O] for i in range(2)]
                cols = [w[:, :, O:W2N].rearrange("p k (j e) -> p k j e", e=2) for w in wo]
                for part, raw in zip(parts, raws):
                    nc.vector.tensor_copy(part[0], raw)
                for e in range(2):
                    ins = nc.vector.tensor_copy(cols[0][:, :, :, e], u_out[:, :, :])
                link(ins)
                for part, raw in zip(parts, raws):
                    nc.vector.tensor_tensor(part[1], raw, part[0], ALU.subtract)
                dve.wait_ge(wo_lo_done, 2)
                for e in range(2):
                    ins = nc.vector.tensor_tensor(cols[1][:, :, :, e], u_out[:, :, :], cols[0][:, :, :, e], ALU.subtract)
                ins.then_inc(out_made, 1)

            def split_xt(p, b):
                dve.wait_ge(xt_hi_done, p * 2 + b + 1)
                nc.vector.tensor_tensor(xt[1][:, :, b, :], bank[BANK[("xt", b)]][:, :].rearrange(
                    "p (c n) -> p c n", c=FC), xt[0][:, :, b, :], ALU.subtract).then_inc(xt_split, 1)

            def x_hi(p):
                dve.wait_ge(x_loaded, p * 16 + 16)
                reach(dve, y_ready, p * 2 * H)
                nc.vector.tensor_copy(xs[0][:, :, :, :].rearrange("p b c f -> p (b c f)"),
                                      xn[:, :, :, :].rearrange("p b c f -> p (b c f)")).then_inc(x_hi_done, 1)

            def factors(p, ly):
                q = p - ly
                rows = FROWS if ly == 0 else 4
                tile = ("f",) if ly == 0 else ("f2",)
                ps = bank[BANK[tile]]
                dve.wait_ge(f_hi_done[ly], q + 1)
                if ly == 0:
                    reach(dve, lr_done[1], p - 1)
                    reach(dve, lr_done[0], p)
                else:
                    dve.wait_ge(lr_done[0], p + 1 if one_now[0] else PAIRS)
                nc.vector.scalar_tensor_tensor(out=f_sp[0:rows, :], in0=f_hi[0:rows, :], scalar=row_w[0:rows, 2:3],
                                               in1=ps[0:rows, :], op0=ALU.mult, op1=ALU.add).then_inc(f_split[ly], 1)
                dve.wait_ge(f_split[ly], q + 1)
                reach(dve, z_ready[ly], q * 2 * H if ly == 0 else q * 2)
                if ly == 0:
                    for h in range(H):
                        nc.vector.tensor_scalar(L[:, h, :], f_sp[:, :], row_sel[0:FROWS, 0, h:h + 1],
                                                row_sel[0:FROWS, 1, h:h + 1], ALU.mult, ALU.add)
                    nc.vector.tensor_scalar(R[:, :], f_sp[:, :], row_w[0:FROWS, 1:2], row_w[0:FROWS, 0:1], ALU.mult,
                                            ALU.add).then_inc(lr_done[0], 1)
                else:
                    nc.vector.tensor_scalar(L2[0:4, :], f_sp[0:4, :], row_sel[0:4, 0, 0:1], row_sel[0:4, 1, 0:1],
                                            ALU.mult, ALU.add)
                    nc.vector.tensor_scalar(R2[0:4, :], f_sp[0:4, :], row_w[0:4, 1:2], row_w[0:4, 0:1], ALU.mult,
                                            ALU.add).then_inc(lr_done[1], 1)

            def logits(p, b, h):
                ly, s = layer_of(h), att_slot(h)
                reach_alone(dve, (u_made, 1), (relu_done[ly], item(ly, p - ly, b, h)))
                ps = bank[BANK[("z", b, h)]]
                for c in range(NC):
                    ins = nc.vector.tensor_tensor_reduce(att[:, s, b, c, :], ps[:, c * N:(c + 1) * N],
                                                         att[:, s, b, c, :], -1.0, 3.0e38, ALU.add, ALU.min,
                                                         negmax[:, s, b, c:c + 1])
                ins.then_inc(logits_done[ly], 1)

            def normalize(p, b, h):
                ly, s = layer_of(h), att_slot(h)
                n = item(ly, p - ly, b, h)
                dve.wait_ge(exp_done[ly], n)
                nc.vector.reciprocal(inv[:, s, b, :], total[:, s, b, :]).then_inc(inv_done[ly], 1)
                dve.wait_ge(inv_done[ly], n)
                for c in range(NC):
                    ins = nc.vector.tensor_scalar(att[:, s, b, c, :], att[:, s, b, c, :], inv[:, s, b, c:c + 1], None,
                                                  ALU.mult)
                ins.then_inc(probs_done[ly], 1)

            def pt_lo(p, b, h):
                ly = layer_of(h)
                dve.wait_ge(pt_hi_done[ly], item(ly, p - ly, b, h))
                dst = [t[:, pt_slot(h), b, :, :].rearrange("p c n -> p (c n)") for t in pt]
                nc.vector.tensor_tensor(dst[1], bank[BANK[("t", b, h)]][:, :], dst[0], ALU.subtract).then_inc(pt_lo_done[ly], 1)

            def y_lo(p, b, h):
                dve.wait_ge(y_hi_done, item(0, p, b, h))
                nc.vector.tensor_tensor(yt[1][:, h % 2, :, b, :], bank[BANK[("y", b, h)]][:, :].rearrange(
                    "p (c n) -> p c n", c=FC), yt[0][:, h % 2, :, b, :], ALU.subtract).then_inc(y_lo_done, 1)

            def elu(p, h, oc):
                i = OC * h + oc
                dve.wait_ge(w_neg, p * KC + i + 1)
                nc.vector.scalar_tensor_tensor(out=elu_w[:, i % 4, :], in0=bank[BANK[("w", h, oc)]][:, :], scalar=0.0,
                                               in1=elu_w[:, i % 4, :], op0=ALU.max, op1=ALU.subtract).then_inc(w_elu, 1)

            def v_lo_(p, b, mc):
                dve.wait_ge(v_hi, (p - 1) * 4 + 2 * b + mc + 1)
                dve.wait_ge(f2_cols, (p - 1) * 4 + 2 * b + mc + 1)
                nc.vector.tensor_tensor(v[1][:, b, mc, :], bank[BANK[("v", b, mc)]][:, 0:O], v[0][:, b, mc, :],
                                        ALU.subtract).then_inc(v_lo, 1)

            def elu_out(p, oc):
                q = p - 1
                dve.wait_ge(o_neg, q * 2 + oc + 1)
                nc.vector.scalar_tensor_tensor(out=elu_o[:, oc, :], in0=bank[BANK[("o", oc)]][:, :], scalar=0.0,
                                               in1=elu_o[:, oc, :], op0=ALU.max, op1=ALU.subtract).then_inc(o_elu, 1)

            def norm_stats(p, b):
                q = p - 1
                n = q * 2 + b + 1
                ps = bank[BANK[("r", b)]]
                dve.wait_ge(r_ready, n)
                for c in range(NC):
                    ins = nc.vector.bn_stats(bn1[:, b, c, :], ps[:, c * O:(c + 1) * O])
                ins.then_inc(bn1_done, 1)
                reach_alone(dve, (u_made, 1), (bn1_done, n))
                for c in range(NC):
                    ins = nc.vector.bn_aggr(mv1[:, b, c, :], bn1[:, b, c, :])
                ins.then_inc(mv1_done, 1)
                dve.wait_ge(mv1_done, n)
                reach(dve, stored, q * 32)
                for c in range(NC):
                    ins = nc.vector.scalar_tensor_tensor(out=ln[:, b, c, :], in0=ps[:, c * O:(c + 1) * O],
                                                         scalar=mv1[:, b, c, 0:1], in1=gamma_b[:, :],
                                                         op0=ALU.subtract, op1=ALU.mult)
                ins.then_inc(scaled, 1)

            def add_residual(p, b):
                q = p - 1
                n = q * 2 + b + 1
                dve.wait_ge(rs1_done, n)
                dve.wait_ge(scaled, n)
                dve.wait_ge(xres_ready, q + 1)
                for c in range(NC):
                    ins = nc.vector.scalar_tensor_tensor(out=ln[:, b, c, :], in0=ln[:, b, c, :],
                                                         scalar=rs1[:, b, c:c + 1], in1=xres[:, b, c, :],
                                                         op0=ALU.mult, op1=ALU.add)
                ins.then_inc(ln1_done, 1)
                dve.wait_ge(ln1_done, n)
                for c in range(NC):
                    ins = nc.vector.bn_stats(bn2[:, b, c, :], ln[:, b, c, :])
                ins.then_inc(bn2_done, 1)
                reach_alone(dve, (u_made, 1), (bn2_done, n))
                for c in range(NC):
                    ins = nc.vector.bn_aggr(mv2[:, b, c, :], bn2[:, b, c, :])
                ins.then_inc(mv2_done, 1)

            def second_norm(p, b):
                n = (p - 1) * 2 + b + 1
                dve.wait_ge(rs2_done, n)
                for c in range(NC):
                    ins = nc.vector.tensor_scalar(ln[:, b, c, :], ln[:, b, c, :], mv2[:, b, c, 0:1],
                                                  rs2[:, b, c:c + 1], ALU.subtract, ALU.mult)
                ins.then_inc(ln2_done, 1)

            one_now = [True]

            def step(p, one, two):
                one_now[0] = one
                first = isinstance(p, int) and p == 0
                if one:
                    split_xt(p, 0), split_xt(p, 1)
                if two:
                    v_lo_(p, 0, 0)
                if one:
                    factors(p, 0)
                    if first:
                        split_w_heads()
                if two:
                    v_lo_(p, 0, 1)
                if one:
                    x_hi(p), logits(p, 0, 0), logits(p, 1, 0), logits(p, 0, 1), normalize(p, 0, 0)
                    normalize(p, 1, 0), logits(p, 1, 1), normalize(p, 0, 1), logits(p, 0, 2), pt_lo(p, 0, 0)
                if two:
                    v_lo_(p, 1, 0)
                if one:
                    pt_lo(p, 1, 0), normalize(p, 1, 1), logits(p, 1, 2)
                if two:
                    factors(p, 1)
                if one:
                    pt_lo(p, 0, 1)
                if two:
                    v_lo_(p, 1, 1)
                if one:
                    y_lo(p, 0, 0)
                if two:
                    logits(p, 0, H)
                if one:
                    y_lo(p, 1, 0), pt_lo(p, 1, 1)
                if two:
                    logits(p, 1, H), normalize(p, 0, H)
                if one:
                    normalize(p, 0, 2)
                if two:
                    normalize(p, 1, H)
                if one:
                    normalize(p, 1, 2)
                if two:
                    pt_lo(p, 0, H), pt_lo(p, 1, H)
                if one:
                    logits(p, 0, 3), elu(p, 0, 0), pt_lo(p, 0, 2), y_lo(p, 0, 1), y_lo(p, 1, 1)
                    if first:
                        out_columns(0)
                if two:
                    elu_out(p, 0)
                if one:
                    normalize(p, 0, 3), pt_lo(p, 1, 2)
                if two:
                    elu_out(p, 1)
                if one:
                    elu(p, 0, 1), y_lo(p, 0, 2), logits(p, 1, 3), pt_lo(p, 0, 3), elu(p, 1, 0)
                    y_lo(p, 1, 2)
                    if first:
                        out_columns(1)
                    normalize(p, 1, 3), elu(p, 1, 1), y_lo(p, 0, 3)
                    if first:
                        split_ffn()
                    pt_lo(p, 1, 3), elu(p, 2, 0)
                if two:
                    norm_stats(p, 0)
                if one:
                    y_lo(p, 1, 3)
                if two:
                    add_residual(p, 0), norm_stats(p, 1)
                if one:
                    elu(p, 2, 1), elu(p, 3, 0)
                if two:
                    add_residual(p, 1)
                if one:
                    elu(p, 3, 1)
                if two:
                    second_norm(p, 0), second_norm(p, 1)

            set_up()
            step(0, True, False)
            step(1, True, True)
            with dve.Fori(2, PAIRS) as p:
                step(p, True, True)
            step(PAIRS, False, True)


_INS = ['x', 'adj', 'L0_gnn_W_heads', 'L0_gnn_a_heads', 'L0_gnn_W_out', 'L0_gnn_a_out', 'L0_gnn_w1', 'L0_gnn_b1',
        'L0_gnn_w2', 'L0_gnn_b2', 'L0_gnn_ln_gamma', 'L0_gnn_ln_beta']
_OUTS = [((32, 256, 256), 'float32')]


def kernel(**inputs):
    import numpy as _np
    import concourse.bacc as _bacc
    from concourse import mybir as _mybir
    from concourse.bass_utils import run_bass_kernel_spmd as _run

    nc = _bacc.Bacc("TRN2", target_bir_lowering=False, num_devices=1)
    arrays, args = {}, []
    for name in _INS:
        a = _np.ascontiguousarray(inputs[name])
        arrays[f"in_{name}_dram"] = a
        args.append(nc.dram_tensor(f"in_{name}_dram", a.shape, _mybir.dt.from_np(a.dtype), kind="ExternalInput").ap())
    for i, (shape, dtype) in enumerate(_OUTS):
        dt = _mybir.dt.from_np(_np.dtype(dtype))
        args.append(nc.dram_tensor(f"out_{i}_dram", shape, dt, kind="ExternalOutput").ap())
    gat_block(nc, *args)
    r = _run(nc, [arrays], core_ids=[0])
    got = tuple(r.results[0][f"out_{i}_dram"] for i in range(len(_OUTS)))
    return got[0]
```

```python
from contextlib import ExitStack

import concourse.bass as bass
from concourse import mybir

F32 = mybir.dt.float32
F32R = mybir.dt.float32r
BF16 = mybir.dt.bfloat16
I32 = mybir.dt.int32
ACT = mybir.ActivationFunctionType
ALU = mybir.AluOpType
AX = mybir.AxisListType

P = 128
SLOPE = 0.01
MASKED = -1.0e9
EPS = 1e-5


def gat_block(nc: bass.Bass, x, adj, w_heads, a_heads, w_out, a_out, w1, b1, w2, b2, gamma, beta, out):
    B, N, F = x.shape
    H, _, O = w_heads.shape
    PAIRS = B // 2
    NC = N // P
    FC = F // P
    OC = O // P
    KC = H * OC
    FCOLS = 4
    W2N = O + FCOLS
    HROWS = P // H
    assert N == F == O == 256 and H == 4 and w_out.shape == (H * O, O) and w1.shape == (O, O)

    ctx = ExitStack()
    with ctx:
        def sb(name, shape, dt):
            return ctx.enter_context(nc.sbuf_tensor(name, shape, dt))

        def sem(name):
            return ctx.enter_context(nc.semaphore(name))

        ident = sb("ident", [P, P], F32)
        ident_b = sb("ident_b", [P, P], BF16)
        ident_r = sb("ident_r", [P, P], F32R)
        ones_r = sb("ones_r", [P, P], F32R)
        mask = sb("mask", [P, NC, N], BF16)
        row_sel = sb("row_sel", [P, 3, H, 2], F32)
        row_w = sb("row_w", [P, 3], F32)
        wh = [sb(f"wh_{s}", [P, FC, H, O], F32R) for s in ("hi", "lo")]
        wo = [sb(f"wo_{s}", [P, KC, W2N], F32R) for s in ("hi", "lo")]
        w1s = [sb(f"w1_{s}", [P, OC, O], F32R) for s in ("hi", "lo")]
        w2s = [sb(f"w2_{s}", [P, OC, O], F32R) for s in ("hi", "lo")]
        u_in = [sb(f"u_in_{s}", [P, FC, P], F32R) for s in ("hi", "lo")]
        u_out = sb("u_out", [P, KC, 2], F32)
        u_sum = sb("u_sum", [P, FC, 2 * H], F32)
        b1c = sb("b1c", [P, OC], F32)
        b2r = sb("b2r", [P, O], F32R)
        gamma_b = sb("gamma_b", [P, O], F32)
        beta_b = sb("beta_b", [P, O], F32)
        eps_c = sb("eps_c", [P, NC], F32)
        minus_half = sb("minus_half", [P, NC], F32)

        xn = sb("xn", [P, 2, NC, F], F32)
        xs = [sb(f"x_{s}", [P, 2, NC, F], F32R) for s in ("hi", "lo")]
        xt = [sb(f"xt_{s}", [P, FC, 2, N], F32R) for s in ("hi", "lo")]
        f_hi = sb("f_hi", [P, 2 * N], F32R)
        f_sp = sb("f_sp", [P, 2 * N], F32R)
        L = sb("L", [P, 2 * N], F32R)
        R = sb("R", [P, 2 * N], F32R)
        att = sb("att", [P, 4, 2, NC, N], F32)
        negmax = sb("negmax", [P, 4, 2, NC], F32)
        total = sb("total", [P, 4, 2, NC], F32)
        inv = sb("inv", [P, 4, 2, NC], F32)
        pt = [sb(f"pt_{s}", [P, 2, 2, NC, N], F32R) for s in ("hi", "lo")]
        yt = [sb(f"yt_{s}", [P, 2, FC, 2, N], F32R) for s in ("hi", "lo")]
        elu_w = sb("elu_w", [P, 4, 2 * N], F32)
        ht = [sb(f"ht_{s}", [P, KC, 2 * N], F32R) for s in ("hi", "lo")]
        v = [sb(f"v_{s}", [P, 2, NC, O], F32R) for s in ("hi", "lo")]
        f2pad = sb("f2pad", [P, 2, NC, P], F32)
        L2 = sb("L2", [P, 2 * N], F32R)
        R2 = sb("R2", [P, 2 * N], F32R)
        elu_o = sb("elu_o", [P, OC, 2 * N], F32)
        ot = [sb(f"ot_{s}", [P, OC, 2 * N], F32R) for s in ("hi", "lo")]
        rt = [sb(f"rt_{s}", [P, OC, 2 * N], F32R) for s in ("hi", "lo")]
        xres = sb("xres", [P, 2, NC, O], F32)
        ln = sb("ln", [P, 2, NC, O], F32)
        bn1 = sb("bn1", [P, 2, NC, 6], F32)
        mv1 = sb("mv1", [P, 2, NC, 2], F32)
        ve1 = sb("ve1", [P, 2, NC], F32)
        rs1 = sb("rs1", [P, 2, NC], F32)
        bn2 = sb("bn2", [P, 2, NC, 6], F32)
        mv2 = sb("mv2", [P, 2, NC, 2], F32)
        ve2 = sb("ve2", [P, 2, NC], F32)
        rs2 = sb("rs2", [P, 2, NC], F32)

        bank = [ctx.enter_context(nc.psum_tensor(f"bank{i}", [P, 512], F32)) for i in range(8)]
        BANK = dict([(("z", 0, 0), 5), (("z", 1, 0), 7), (("v", 0, 0), 2), (("z", 0, 1), 5), (("z", 1, 1), 6),
                     (("v", 0, 1), 0), (("z", 0, 2), 1), (("z", 1, 2), 5), (("f2", 0), 7), (("t", 0, 0), 3),
                     (("v", 1, 0), 4), (("t", 1, 0), 1), (("z", 0, 3), 6), (("t", 0, 1), 2), (("v", 1, 1), 3),
                     (("z", 0, H), 5), (("y", 0, 0), 1), (("t", 1, 1), 4), (("z", 1, 3), 6), (("f2", 1), 5),
                     (("y", 1, 0), 2), (("y", 0, 1), 7), (("t", 0, 2), 1), (("z", 1, H), 0), (("xt", 0), 2),
                     (("y", 1, 1), 5), (("t", 0, H), 3), (("w", 0, 0), 7), (("t", 1, 2), 6), (("w", 0, 1), 0),
                     (("o", 0), 3), (("y", 0, 2), 4), (("t", 0, 3), 2), (("xt", 1), 5), (("t", 1, H), 7),
                     (("w", 1, 0), 1), (("y", 1, 2), 0), (("o", 1), 4), (("w", 1, 1), 3), (("t", 1, 3), 6),
                     (("g", 0), 7), (("y", 0, 3), 2), (("w", 2, 0), 1), (("w", 2, 1), 0), (("f",), 4),
                     (("y", 1, 3), 7), (("g", 1), 2), (("r", 0), 5), (("w", 3, 0), 7), (("w", 3, 1), 1),
                     (("r", 1), 4)])

        def reach(eng, s, value):
            if not (isinstance(value, int) and value <= 0):
                eng.wait_ge(s, value)

        def reach_alone(eng, known, *counts):
            for s, n in counts:
                if not isinstance(n, int):
                    eng.compute_val(n)
            eng.wait_ge(*known)
            for s, n in counts:
                reach(eng, s, n)

        def graph(t, b):
            return t[:, :, b * N:(b + 1) * N]

        def halves(ps):
            return ps[:, :].rearrange("p (c n) -> p c n", n=N)

        def att_slot(h):
            return {0: 0, 1: 1, 2: 2, 3: 0, H: 3}[h]

        def pt_slot(h):
            return {0: 0, 1: 1, H: 0, 2: 1, 3: 0}[h]

        wh_loaded = [sem(f"wh{c}_loaded") for c in range(FC)]
        ah_loaded = [sem(f"ah{i}_loaded") for i in range(2)]
        adj_loaded, wo_loaded = (sem(f"{s}_loaded") for s in ("adj", "wo"))
        w12_loaded, b2_loaded, vectors_loaded = sem("w12_loaded"), sem("b2_loaded"), sem("vectors_loaded")
        consts_made, masks_made, u_made = sem("consts_made"), sem("masks_made"), sem("u_made")
        w12_hi_done, w12_split = sem("w12_hi_done"), sem("w12_split")
        wh_hi_done, wh_split, wo_hi_done, wo_lo_done, out_made = (
            sem(s) for s in ("wh_hi_done", "wh_split", "wo_hi_done", "wo_lo_done", "out_made"))
        dve_chain, pool_chain = sem("dve_chain"), sem("pool_chain")
        x_loaded = sem("x_loaded")
        xt_ready, xt_hi_done, xt_split = sem("xt_ready"), sem("xt_hi_done"), sem("xt_split")
        x_hi_done, x_lo_done = sem("x_hi_done"), sem("x_lo_done")
        f_ready = [sem("f1_ready"), sem("f2_ready")]
        f_hi_done = [sem("f1_hi_done"), sem("f2_hi_done")]
        f_split = [sem("f1_split"), sem("f2_split")]
        lr_done = [sem("lr1_done"), sem("lr2_done")]
        z_ready = [sem("z1_ready"), sem("z2_ready")]
        relu_done = [sem("relu1_done"), sem("relu2_done")]
        logits_done = [sem("logits1_done"), sem("logits2_done")]
        exp_done = [sem("exp1_done"), sem("exp2_done")]
        inv_done = [sem("inv1_done"), sem("inv2_done")]
        probs_done = [sem("probs1_done"), sem("probs2_done")]
        t_ready = [sem("t1_ready"), sem("t2_ready")]
        pt_hi_done = [sem("pt1_hi_done"), sem("pt2_hi_done")]
        pt_lo_done = [sem("pt1_lo_done"), sem("pt2_lo_done")]
        y_ready, y_hi_done, y_lo_done = sem("y_ready"), sem("y_hi_done"), sem("y_lo_done")
        w_ready = sem("w_ready")
        w_exp, w_neg, w_elu, w_hi, w_lo = (sem(f"w_{s}") for s in ("exp", "neg", "elu", "hi", "lo"))
        v_ready, v_hi, v_lo, f2_cols = (sem(s) for s in ("v_ready", "v_hi_done", "v_lo_done", "f2_cols"))
        o_ready = sem("o_ready")
        o_exp, o_neg, o_elu, o_hi, o_lo = (sem(f"o_{s}") for s in ("exp", "neg", "elu", "hi", "lo"))
        g_ready, g_hi, g_lo = (sem(f"g_{s}") for s in ("ready", "hi", "lo"))
        r_ready = sem("r_ready")
        xres_loaded, xres_ready = sem("xres_loaded"), sem("xres_ready")
        bn1_done, mv1_done, ve1_done, rs1_done = (sem(s) for s in ("bn1_done", "mv1_done", "ve1_done", "rs1_done"))
        scaled, ln1_done = sem("scaled"), sem("ln1_done")
        bn2_done, mv2_done, ve2_done, rs2_done = (sem(s) for s in ("bn2_done", "mv2_done", "ve2_done", "rs2_done"))
        ln2_done = sem("ln2_done")
        stored = sem("stored")

        def item(layer, pair, b, h):
            return pair * (2 * H) + 2 * h + b + 1 if layer == 0 else pair * 2 + b + 1

        def layer_of(h):
            return 1 if h == H else 0

        def read_out(tile, p):
            kind, at = tile[0], tile[1:]
            q = p - 1
            if kind in "zt":
                ly = layer_of(at[1])
                return (logits_done if kind == "z" else pt_lo_done)[ly], item(ly, p - ly, *at)
            if kind == "xt":
                return xt_split, p * 2 + at[0] + 1
            if kind == "f":
                return f_split[0], p + 1
            if kind == "f2":
                return f_split[1], q * 2 + at[0] + 1
            if kind == "y":
                return y_lo_done, item(0, p, *at)
            if kind == "w":
                return w_elu, p * KC + OC * at[0] + at[1] + 1
            if kind == "v":
                return v_lo, q * 4 + 2 * at[0] + at[1] + 1
            return {"o": o_elu, "g": g_hi, "r": scaled}[kind], q * 2 + at[0] + 1

        x_rows = x.rearrange("b (c n) f -> n (b c) f", n=P)
        out_rows = out.rearrange("b (c n) f -> n (b c) f", n=P)

        raw_wh = [t[:, :, :, :].rearrange("p b c o -> p (b c o)") for t in (xres, ln)]
        raw_w12 = raw_wh[0]
        raw_ao = raw_wh[1][:, 0:2 * O]
        raw_ah = att[:, 0:2, :, :, :].rearrange("p s b c m -> p (s b c m)")
        raw_wo = [att[:, 3, :, :, :].rearrange("p b c m -> p (b c m)"), elu_o[:, :, :].rearrange("p c n -> p (c n)")]
        raw_adj, raw_b2, b2_hi = elu_w[:, 0, :].bitcast(I32), elu_w[0:2, 1, 0:O], elu_w[0:2, 1, O:2 * O].bitcast(F32R)
        junk_in = [elu_w[:, 2 + i // 2, (i % 2) * O:(i % 2 + 1) * O] for i in range(4)]
        junk_out = [raw_wh[1][:, (2 + i) * O:(3 + i) * O] for i in range(2)]

        block = ctx.enter_context(nc.Block())

        @block.sync
        def _(sp):
            for c in range(FC):
                sp.dma_start(raw_wh[c].rearrange("p (h o) -> p h o", h=H),
                             w_heads[:, c * P:(c + 1) * P, :].rearrange("h f o -> f h o")).then_inc(wh_loaded[c], 16)
                if c == FC - 1:
                    sp.dma_start(xn[:, :, :, :].rearrange("p b c f -> p (b c) f"),
                                 x_rows[:, 0:2 * NC, :]).then_inc(x_loaded, 16)
            sp.wait_ge(ah_loaded[1], 16)
            sp.dma_start(raw_wo[0].rearrange("p (k o) -> p k o", o=O),
                         w_out[0:KC * P // 2, :].rearrange("(k p) o -> p k o", p=P)).then_inc(wo_loaded, 16)
            sp.dma_start(raw_wo[1].rearrange("p (k o) -> p k o", o=O),
                         w_out[KC * P // 2:KC * P, :].rearrange("(k p) o -> p k o", p=P)).then_inc(wo_loaded, 16)

            def load_next(p):
                reach_alone(sp, (x_loaded, 16), (xt_ready, p * 2 + 2), (x_hi_done, p + 1), (x_lo_done, p + 1))
                sp.dma_start(xn[:, :, :, :].rearrange("p b c f -> p (b c) f"),
                             x_rows[:, bass.ds(p * (2 * NC) + 2 * NC, 2 * NC), :]).then_inc(x_loaded, 16)

            def load_residual(q):
                reach_alone(sp, (x_loaded, 16), (ln1_done, q * 2))
                sp.dma_start(xres[:, :, :, :].rearrange("p b c f -> p (b c) f"),
                             x_rows[:, bass.ds(q * (2 * NC), 2 * NC), :]).then_inc(xres_loaded, 16)

            def store(q):
                for b in range(2):
                    reach_alone(sp, (x_loaded, 16), (ln2_done, q * 2 + b + 1))
                    sp.dma_start(out_rows[:, bass.ds(q * (2 * NC) + b * NC, NC), :], ln[:, b, :, :]).then_inc(stored, 16)

            load_next(0)
            sp.wait_ge(wh_split, 1)
            for i, w in enumerate((w1, w2)):
                sp.dma_start(raw_w12[:, i * OC * O:(i + 1) * OC * O].rearrange("p (c o) -> p c o", c=OC),
                             w.rearrange("(c p) o -> p c o", p=P)).then_inc(w12_loaded, 16)
            sp.dma_start(raw_ao, a_out.partition_broadcast(P)).then_inc(vectors_loaded, 16)
            sp.wait_ge(w12_split, 1)
            load_residual(0)
            load_next(1)
            with sp.Fori(2, PAIRS - 1) as p:
                load_next(p)
                load_residual(p - 1)
                store(p - 2)
            for p in (PAIRS - 1, PAIRS):
                load_residual(p - 1)
                store(p - 2)
            store(PAIRS - 1)
            sp.wait_ge(stored, PAIRS * 32)

        @block.gpsimd
        def _(pool):
            def link(ins, n):
                ins.then_inc(pool_chain, 1)
                pool.wait_ge(pool_chain, n)

            link(nc.gpsimd.memset(ident[:, :], 0.0), 1)
            link(nc.gpsimd.affine_select(out=ident[:, :], in_=ident[:, :], compare_op=ALU.not_equal, fill=1.0,
                                         base=0, pattern=[[-1, P]], channel_multiplier=1), 2)
            link(nc.gpsimd.memset(row_sel[:, :, :, :], 0.0), 3)
            for kind, start, stride, fill in ((0, 0, 1, 1.0), (1, 2, 1, 1.0), (2, 1, 2, -1.0)):
                sel = row_sel[:, kind, :, :]
                link(nc.gpsimd.affine_select(out=sel, in_=sel, compare_op=ALU.not_equal, fill=fill, base=-start,
                                             pattern=[[-HROWS, H], [-stride, 2]], channel_multiplier=1), 4 + kind)
            nc.gpsimd.memset(eps_c[:, :], EPS)
            nc.gpsimd.memset(minus_half[:, :], -0.5).then_inc(consts_made, 1)

            def x_lo(p):
                pool.wait_ge(x_hi_done, p + 1)
                nc.gpsimd.tensor_tensor(xs[1][:, :, :, :], xn[:, :, :, :], xs[0][:, :, :, :],
                                        ALU.subtract).then_inc(x_lo_done, 1)

            def h_lo(p, h, oc):
                pool.wait_ge(w_hi, p * KC + OC * h + oc + 1)
                s = (OC * h + oc) % 4
                nc.gpsimd.tensor_tensor(ht[1][:, OC * h + oc, :], elu_w[:, s, :], ht[0][:, OC * h + oc, :],
                                        ALU.subtract).then_inc(w_lo, 1)

            def split_w_heads():
                pool.wait_ge(wh_hi_done, 1)
                for c in range(FC):
                    ins = nc.gpsimd.tensor_tensor(wh[1][:, c, :, :].rearrange("p h o -> p (h o)"), raw_wh[c],
                                                  wh[0][:, c, :, :].rearrange("p h o -> p (h o)"), ALU.subtract)
                ins.then_inc(wh_split, 1)

            def split_ffn_low():
                pool.wait_ge(w12_hi_done, 1)
                for i, w in enumerate((w1s, w2s)):
                    part = [t[:, :, :].rearrange("p c o -> p (c o)") for t in w]
                    ins = nc.gpsimd.tensor_tensor(part[1], raw_w12[:, i * OC * O:(i + 1) * OC * O], part[0],
                                                  ALU.subtract)
                ins.then_inc(w12_split, 1)

            def split_w_out():
                pool.wait_ge(wo_hi_done, 1)
                for j in range(2):
                    nc.gpsimd.tensor_tensor(wo[1][:, 4 * j:4 * j + 4, 0:O],
                                            raw_wo[j].rearrange("p (k o) -> p k o", o=O),
                                            wo[0][:, 4 * j:4 * j + 4, 0:O], ALU.subtract).then_inc(wo_lo_done, 1)

            def residual(q):
                pool.wait_ge(xres_loaded, q * 16 + 16)
                nc.gpsimd.tensor_tensor(xres[:, :, :, :].rearrange("p b c o -> p (b c) o"),
                                        xres[:, :, :, :].rearrange("p b c o -> p (b c) o"),
                                        beta_b[:, :].unsqueeze(1).broadcast_to([P, 2 * NC, O]),
                                        ALU.add).then_inc(xres_ready, 1)

            def o_lo_(q, b):
                pool.wait_ge(o_hi, q * 2 + b + 1)
                nc.gpsimd.tensor_tensor(graph(ot[1], b), graph(elu_o, b), graph(ot[0], b),
                                        ALU.subtract).then_inc(o_lo, 1)

            def r_lo_(q, b):
                pool.wait_ge(g_hi, q * 2 + b + 1)
                nc.gpsimd.tensor_tensor(graph(rt[1], b), graph(elu_o, b), graph(rt[0], b),
                                        ALU.subtract).then_inc(g_lo, 1)

            def rstd(q, b, mv, ve, rs, mv_done, ve_done, rs_done):
                pool.wait_ge(mv_done, q * 2 + b + 1)
                nc.gpsimd.tensor_tensor(ve[:, b, :], mv[:, b, :, 1], eps_c[:, :], ALU.add).then_inc(ve_done, 1)
                pool.wait_ge(ve_done, q * 2 + b + 1)
                nc.gpsimd.tensor_tensor(rs[:, b, :], ve[:, b, :], minus_half[:, :], ALU.pow).then_inc(rs_done, 1)

            def rstd1(q, b):
                rstd(q, b, mv1, ve1, rs1, mv1_done, ve1_done, rs1_done)

            def rstd2(q, b):
                rstd(q, b, mv2, ve2, rs2, mv2_done, ve2_done, rs2_done)

            def first_step():
                x_lo(0), split_w_heads(), h_lo(0, 0, 0), split_w_out(), h_lo(0, 0, 1), h_lo(0, 1, 0)
                h_lo(0, 1, 1), h_lo(0, 2, 0), h_lo(0, 2, 1), h_lo(0, 3, 0), h_lo(0, 3, 1), split_ffn_low()

            def step(p, pre, one, two, post):
                q = p - 1
                if one:
                    x_lo(p)
                if post:
                    rstd2(p - 2, 0)
                if two:
                    o_lo_(q, 0)
                if one:
                    h_lo(p, 0, 0), h_lo(p, 0, 1)
                if post:
                    rstd2(p - 2, 1)
                if one:
                    h_lo(p, 1, 0)
                if two:
                    o_lo_(q, 1), r_lo_(q, 0)
                if one:
                    h_lo(p, 1, 1)
                if two:
                    residual(q), r_lo_(q, 1)
                if one:
                    h_lo(p, 2, 0), h_lo(p, 2, 1)
                if two:
                    rstd1(q, 0)
                if one:
                    h_lo(p, 3, 0), h_lo(p, 3, 1)
                if two:
                    rstd1(q, 1)

            def last_step():
                rstd2(PAIRS - 2, 0), o_lo_(PAIRS - 1, 0), o_lo_(PAIRS - 1, 1), r_lo_(PAIRS - 1, 0)
                rstd2(PAIRS - 2, 1), r_lo_(PAIRS - 1, 1), residual(PAIRS - 1), rstd1(PAIRS - 1, 0)
                rstd1(PAIRS - 1, 1)

            first_step()
            step(1, True, True, True, False)
            with pool.Fori(2, PAIRS - 1) as p:
                step(p, True, True, True, True)
            step(PAIRS - 1, False, True, True, True)
            last_step()
            step(PAIRS + 1, False, False, False, True)

        @block.tensor
        def _(pe):
            held, before, now = {}, {}, [0]

            def next_step(p):
                before.clear()
                before.update((b, tile) for b, (tile, _) in held.items())
                held.clear()
                now[0] = p

            def take(tile, p):
                b = BANK[tile]
                if b in held:
                    pe.wait_ge(*read_out(*held[b]))
                elif b in before:
                    reach(pe, *read_out(before[b], now[0] - 1 + (before[b][0] in ("xt", "f"))))
                held[b] = tile, p
                return bank[b]

            def split_product(ps, lhs, rhs, n, start=True, last_stop=True):
                for i in range(n):
                    for j, (a, b) in enumerate(((0, 0), (1, 0), (0, 1))):
                        mm = nc.tensor.matmul(ps, lhs(a, i), rhs(b, i), start=(start and i == 0 and j == 0),
                                              stop=(last_stop and i == n - 1 and j == 2))
                return mm

            def transpose_x(p, b):
                ps = take(("xt", b), p)
                if b == 0:
                    pe.wait_ge(x_loaded, p * 16 + 16)
                for fc in range(FC):
                    for c in range(NC):
                        mm = nc.tensor.transpose(ps[:, fc * N + c * P:fc * N + (c + 1) * P],
                                                 xn[:, b, c, fc * P:(fc + 1) * P], ident[:, :])
                mm.then_inc(xt_ready, 1)

            def f_rows(p):
                ps = take(("f",), p)
                if isinstance(p, int) and p == 0:
                    pe.wait_ge(u_made, 1)
                pe.wait_ge(xt_split, p * 2 + 2)
                split_product(ps[:, :], lambda s, i: u_in[s][:, i, :],
                              lambda s, i: xt[s][:, i, :, :].rearrange("p b n -> p (b n)"), FC).then_inc(f_ready[0], 1)

            def f2_rows(p, b):
                ps = take(("f2", b), p)
                pe.wait_ge(f2_cols, (p - 1) * 4 + 2 * b + 2)
                for c in range(NC):
                    mm = nc.tensor.transpose(ps[:, c * P:(c + 1) * P], f2pad[:, b, c, :], ident[:, :])
                mm.then_inc(f_ready[1], 1)

            def scores(p, b, h):
                ps = take(("z", b, h), p)
                ly = layer_of(h)
                pe.wait_ge(lr_done[ly], p + 1 if ly == 0 else (p - 1) * 2 + b + 1)
                rows = slice(HROWS * h, HROWS * (h + 1))
                lhs, rhs = (L[rows, :], R[rows, :]) if ly == 0 else (L2, R2)
                if isinstance(p, int) and p == 0 and (b, h) == (0, 0):
                    pe.wait_ge(masks_made, 1)
                nc.tensor.matmul(ps[:, :], ident_b[:, :], mask[:, :, :].rearrange("p c m -> p (c m)"), start=True,
                                 stop=False)
                for c in range(NC):
                    mm = nc.tensor.matmul(ps[:, c * N:(c + 1) * N], lhs[:, b * N + c * P:b * N + (c + 1) * P],
                                          rhs[:, b * N:(b + 1) * N], start=False, stop=(c == NC - 1))
                mm.then_inc(z_ready[ly], 1)

            def transpose_probs(p, b, h):
                ps = take(("t", b, h), p)
                ly = layer_of(h)
                pe.wait_ge(probs_done[ly], item(ly, p - ly, b, h))
                for mc in range(NC):
                    for c in range(NC):
                        mm = nc.tensor.transpose(ps[:, mc * N + c * P:mc * N + (c + 1) * P],
                                                 att[:, att_slot(h), b, c, mc * P:(mc + 1) * P], ident[:, :])
                mm.then_inc(t_ready[ly], 1)

            def attend_x(p, b, h):
                ps = take(("y", b, h), p)
                pe.wait_ge(pt_hi_done[0], item(0, p, b, h))
                pe.wait_ge(pt_lo_done[0], item(0, p, b, h))
                if h == 0 and b == 0:
                    pe.wait_ge(x_lo_done, p + 1)
                for fc in range(FC):
                    mm = split_product(ps[:, fc * N:(fc + 1) * N],
                                       lambda s, i: xs[s][:, b, i, fc * P:(fc + 1) * P],
                                       lambda s, i: pt[s][:, pt_slot(h), b, i, :], NC)
                mm.then_inc(y_ready, 1)

            def project_head(p, h, oc):
                ps = take(("w", h, oc), p)
                if isinstance(p, int) and p == 0 and (h, oc) == (0, 0):
                    pe.wait_ge(wh_split, 1)
                pe.wait_ge(y_hi_done, item(0, p, 1, h))
                pe.wait_ge(y_lo_done, item(0, p, 1, h))
                split_product(ps[:, :], lambda s, i: wh[s][:, i, h, oc * P:(oc + 1) * P],
                              lambda s, i: yt[s][:, h % 2, i, :, :].rearrange("p b n -> p (b n)"),
                              FC).then_inc(w_ready, 1)

            def project_out(p, b, mc):
                ps = take(("v", b, mc), p)
                if isinstance(p, int) and p == 1 and (b, mc) == (0, 0):
                    pe.wait_ge(out_made, 1)
                for k in range(KC):
                    pe.wait_ge(w_lo, (p - 1) * KC + k + 1)
                    for j, (s, t) in enumerate(((0, 0), (1, 0), (0, 1))):
                        mm = nc.tensor.matmul(ps[:, 0:W2N], ht[s][:, k, b * N + mc * P:b * N + (mc + 1) * P],
                                              wo[t][:, k, :], start=(k == 0 and j == 0), stop=(k == KC - 1 and j == 2))
                mm.then_inc(v_ready, 1)

            def attend_out(p, b):
                ps = take(("o", b), p)
                q = p - 1
                pe.wait_ge(v_lo, q * 4 + 2 * b + 2)
                pe.wait_ge(pt_hi_done[1], item(1, q, b, H))
                pe.wait_ge(pt_lo_done[1], item(1, q, b, H))
                for oc in range(OC):
                    mm = split_product(ps[:, oc * N:(oc + 1) * N],
                                       lambda s, i: v[s][:, b, i, oc * P:(oc + 1) * P],
                                       lambda s, i: pt[s][:, pt_slot(H), b, i, :], NC)
                mm.then_inc(o_ready, 1)

            def ffn_in(p, b):
                ps = take(("g", b), p)
                if isinstance(p, int) and p == 1 and b == 0:
                    pe.wait_ge(w12_split, 1)
                pe.wait_ge(o_lo, (p - 1) * 2 + b + 1)
                for dc in range(OC):
                    mm = split_product(ps[:, dc * N:(dc + 1) * N], lambda s, i: w1s[s][:, i, dc * P:(dc + 1) * P],
                                       lambda s, i: ot[s][:, i, b * N:(b + 1) * N], OC)
                mm.then_inc(g_ready, 1)

            def ffn_out(p, b):
                ps = take(("r", b), p)
                pe.wait_ge(g_lo, (p - 1) * 2 + b + 1)
                for c in range(NC):
                    cols = slice(b * N + c * P, b * N + (c + 1) * P)
                    nc.tensor.matmul(ps[:, c * O:(c + 1) * O], ones_r[:, :], b2r[:, :], start=True, stop=False)
                    split_product(ps[:, c * O:(c + 1) * O], lambda s, i: rt[s][:, i, cols],
                                  lambda s, i: w2s[s][:, i, :], OC, start=False, last_stop=False)
                    for oc in range(OC):
                        for s in range(2):
                            mm = nc.tensor.matmul(ps[:, c * O + oc * P:c * O + (oc + 1) * P], ot[s][:, oc, cols],
                                                  ident_r[:, :], start=False, stop=(oc == OC - 1 and s == 1))
                mm.then_inc(r_ready, 1)

            def first_step():
                next_step(0)
                transpose_x(0, 0), transpose_x(0, 1), f_rows(0)
                scores(0, 0, 0), scores(0, 1, 0), scores(0, 0, 1), scores(0, 1, 1), scores(0, 0, 2)
                transpose_probs(0, 0, 0), scores(0, 1, 2), scores(0, 0, 3), transpose_probs(0, 1, 0)
                transpose_probs(0, 0, 1), transpose_probs(0, 1, 1), attend_x(0, 0, 0), attend_x(0, 1, 0)
                attend_x(0, 0, 1), attend_x(0, 1, 1), scores(0, 1, 3), transpose_x(1, 0)
                transpose_probs(0, 0, 2), project_head(0, 0, 0), project_head(0, 0, 1), attend_x(0, 0, 2)
                transpose_x(1, 1), transpose_probs(0, 1, 2), project_head(0, 1, 0), transpose_probs(0, 0, 3)
                project_head(0, 1, 1), transpose_probs(0, 1, 3), attend_x(0, 1, 2), attend_x(0, 0, 3)
                attend_x(0, 1, 3), f_rows(1), project_head(0, 2, 0), project_head(0, 2, 1)
                project_head(0, 3, 0), project_head(0, 3, 1)

            def step(p, pre, one, two, post):
                next_step(p)
                if one:
                    scores(p, 0, 0), scores(p, 1, 0)
                if two:
                    project_out(p, 0, 0)
                if one:
                    scores(p, 0, 1), scores(p, 1, 1)
                if two:
                    project_out(p, 0, 1)
                if one:
                    scores(p, 0, 2), scores(p, 1, 2)
                if two:
                    f2_rows(p, 0)
                if one:
                    transpose_probs(p, 0, 0)
                if two:
                    project_out(p, 1, 0)
                if one:
                    transpose_probs(p, 1, 0), scores(p, 0, 3), transpose_probs(p, 0, 1)
                if two:
                    project_out(p, 1, 1), scores(p, 0, H)
                if one:
                    attend_x(p, 0, 0), transpose_probs(p, 1, 1), scores(p, 1, 3)
                if two:
                    f2_rows(p, 1)
                if one:
                    attend_x(p, 1, 0), attend_x(p, 0, 1), transpose_probs(p, 0, 2)
                if two:
                    scores(p, 1, H)
                if pre:
                    transpose_x(p + 1, 0)
                if one:
                    attend_x(p, 1, 1)
                if two:
                    transpose_probs(p, 0, H)
                if one:
                    project_head(p, 0, 0), transpose_probs(p, 1, 2), project_head(p, 0, 1)
                if two:
                    attend_out(p, 0)
                if one:
                    attend_x(p, 0, 2), transpose_probs(p, 0, 3)
                if pre:
                    transpose_x(p + 1, 1)
                if two:
                    transpose_probs(p, 1, H)
                if one:
                    project_head(p, 1, 0), attend_x(p, 1, 2)
                if two:
                    attend_out(p, 1)
                if one:
                    project_head(p, 1, 1), transpose_probs(p, 1, 3)
                if two:
                    ffn_in(p, 0)
                if one:
                    attend_x(p, 0, 3), project_head(p, 2, 0), project_head(p, 2, 1)
                if pre:
                    f_rows(p + 1)
                if one:
                    attend_x(p, 1, 3)
                if two:
                    ffn_in(p, 1), ffn_out(p, 0)
                if one:
                    project_head(p, 3, 0), project_head(p, 3, 1)
                if two:
                    ffn_out(p, 1)

            def last_step():
                next_step(PAIRS)
                project_out(PAIRS, 0, 0), project_out(PAIRS, 0, 1), f2_rows(PAIRS, 0)
                project_out(PAIRS, 1, 0), scores(PAIRS, 0, H), project_out(PAIRS, 1, 1), f2_rows(PAIRS, 1)
                transpose_probs(PAIRS, 0, H), scores(PAIRS, 1, H), attend_out(PAIRS, 0)
                transpose_probs(PAIRS, 1, H), attend_out(PAIRS, 1), ffn_in(PAIRS, 0), ffn_in(PAIRS, 1)
                ffn_out(PAIRS, 0), ffn_out(PAIRS, 1)

            pe.wait_ge(consts_made, 1)
            first_step()
            step(1, True, True, True, False)
            with pe.Fori(2, PAIRS - 1) as p:
                step(p, True, True, True, True)
            step(PAIRS - 1, False, True, True, True)
            last_step()
            step(PAIRS + 1, False, False, False, True)

        @block.scalar
        def _(act):
            def split_f(p):
                act.wait_ge(f_ready[0], p + 1)
                reach(act, f_split[1], (p - 1) * 2)
                reach(act, f_split[0], p)
                nc.scalar.activation(f_hi[:, :], bank[BANK[("f",)]][:, :], ACT.Copy).then_inc(f_hi_done[0], 1)

            def split_f2(p, b):
                act.wait_ge(f_ready[1], (p - 1) * 2 + b + 1)
                act.wait_ge(f_split[0], p + 1 if one_now[0] else PAIRS)
                nc.scalar.activation(f_hi[0:4, b * N:(b + 1) * N], bank[BANK[("f2", b)]][0:4, 0:N],
                                     ACT.Copy).then_inc(f_hi_done[1], 1)

            def relu_part(p, b, h):
                ly = layer_of(h)
                n = item(ly, p - ly, b, h)
                act.wait_ge(z_ready[ly], n)
                if h == H:
                    reach(act, t_ready[1], (p - 1) * 2)
                else:
                    reach(act, t_ready[0], item(0, p, b, 0) if h == 3 else item(0, p - 1, b, h or 3))
                nc.scalar.activation(att[:, att_slot(h), b, :, :].rearrange("p c m -> p (c m)"),
                                     bank[BANK[("z", b, h)]][:, :], ACT.Relu,
                                     scale=(1.0 - SLOPE) / SLOPE).then_inc(relu_done[ly], 1)

            def exps(p, b, h):
                ly, s = layer_of(h), att_slot(h)
                n = item(ly, p - ly, b, h)
                act.wait_ge(logits_done[ly], n)
                for c in range(NC):
                    ins = nc.scalar.activation(att[:, s, b, c, :], att[:, s, b, c, :], ACT.Exp, scale=-1.0,
                                               bias=negmax[:, s, b, c:c + 1], accum_out=total[:, s, b, c:c + 1])
                ins.then_inc(exp_done[ly], 1)

            def pt_hi(p, b, h):
                ly = layer_of(h)
                act.wait_ge(t_ready[ly], item(ly, p - ly, b, h))
                if h in (0, 2):
                    reach(act, y_ready, item(0, p - 1, b, 3) if h == 0 else item(0, p, b, 1))
                elif h == 1:
                    reach(act, y_ready, item(0, p - 1, b, 2))
                elif h == H:
                    reach(act, y_ready, item(0, p, b, 0) if one_now[0] else PAIRS * 2 * H)
                elif two_now[0]:
                    act.wait_ge(o_ready, (p - 1) * 2 + b + 1)
                else:
                    act.wait_ge(y_ready, item(0, p, b, 0))
                nc.scalar.activation(pt[0][:, pt_slot(h), b, :, :].rearrange("p c n -> p (c n)"),
                                     bank[BANK[("t", b, h)]][:, :], ACT.Copy).then_inc(pt_hi_done[ly], 1)

            def y_hi(p, b, h):
                act.wait_ge(y_ready, item(0, p, b, h))
                reach(act, w_ready, p * KC + OC * (h - 1) if h >= 2 else p * KC - KC + OC * (h + 3))
                nc.scalar.activation(yt[0][:, h % 2, :, b, :], bank[BANK[("y", b, h)]][:, :].rearrange(
                    "p (c n) -> p c n", c=FC), ACT.Copy).then_inc(y_hi_done, 1)

            def copy_xt(p, b):
                act.wait_ge(xt_ready, p * 2 + b + 1)
                reach(act, f_ready[0], p)
                nc.scalar.activation(xt[0][:, :, b, :], bank[BANK[("xt", b)]][:, :].rearrange(
                    "p (c n) -> p c n", c=FC), ACT.Copy).then_inc(xt_hi_done, 1)

            def w_exp_(p, h, oc):
                i = OC * h + oc
                act.wait_ge(w_ready, p * KC + i + 1)
                reach(act, w_lo, p * KC + i + 1 - 4)
                nc.scalar.activation(elu_w[:, i % 4, :], bank[BANK[("w", h, oc)]][:, :], ACT.Exp).then_inc(w_exp, 1)

            def w_neg_(p, h, oc):
                i = OC * h + oc
                act.wait_ge(w_exp, p * KC + i + 1)
                nc.scalar.activation(elu_w[:, i % 4, :], elu_w[:, i % 4, :], ACT.Relu, scale=-1.0,
                                     bias=1.0).then_inc(w_neg, 1)

            def h_hi(p, h, oc):
                i = OC * h + oc
                act.wait_ge(w_elu, p * KC + i + 1)
                if i == 0:
                    reach(act, v_ready, p * 4)
                nc.scalar.activation(ht[0][:, i, :], elu_w[:, i % 4, :], ACT.Copy).then_inc(w_hi, 1)

            def v_hi_(p, b, mc):
                q = p - 1
                i = 2 * b + mc
                act.wait_ge(v_ready, q * 4 + i + 1)
                reach(act, o_ready, q * 2)
                reach(act, f_ready[1], q * 2)
                ps = bank[BANK[("v", b, mc)]]
                nc.scalar.activation(v[0][:, b, mc, :], ps[:, 0:O], ACT.Copy).then_inc(v_hi, 1)
                nc.scalar.activation(f2pad[:, b, mc, 0:FCOLS], ps[:, O:W2N], ACT.Copy).then_inc(f2_cols, 1)

            def o_exp_(p, b):
                q = p - 1
                act.wait_ge(o_ready, q * 2 + b + 1)
                reach(act, g_lo, q * 2)
                nc.scalar.activation(graph(elu_o, b), halves(bank[BANK[("o", b)]]), ACT.Exp).then_inc(o_exp, 1)

            def o_neg_(p, b):
                q = p - 1
                act.wait_ge(o_exp, q * 2 + b + 1)
                nc.scalar.activation(graph(elu_o, b), graph(elu_o, b), ACT.Relu, scale=-1.0, bias=1.0).then_inc(o_neg, 1)

            def o_hi_(p, b):
                q = p - 1
                act.wait_ge(o_elu, q * 2 + b + 1)
                reach(act, r_ready, q * 2)
                nc.scalar.activation(graph(ot[0], b), graph(elu_o, b), ACT.Copy).then_inc(o_hi, 1)

            def ffn_relu(p, b):
                q = p - 1
                act.wait_ge(g_ready, q * 2 + b + 1)
                for dc in range(OC):
                    nc.scalar.activation(elu_o[:, dc, b * N:(b + 1) * N], bank[BANK[("g", b)]][:, dc * N:(dc + 1) * N],
                                         ACT.Relu, bias=b1c[:, dc:dc + 1])

            def ffn_relu_hi(p, b):
                for dc in range(OC):
                    ins = nc.scalar.activation(rt[0][:, dc, b * N:(b + 1) * N],
                                               bank[BANK[("g", b)]][:, dc * N:(dc + 1) * N], ACT.Relu,
                                               bias=b1c[:, dc:dc + 1])
                ins.then_inc(g_hi, 1)

            def w_heads_hi():
                for c in range(FC):
                    act.wait_ge(wh_loaded[c], 16)
                    ins = nc.scalar.activation(wh[0][:, c, :, :].rearrange("p h o -> p (h o)"), raw_wh[c], ACT.Copy)
                ins.then_inc(wh_hi_done, 1)

            def w_out_hi():
                act.wait_ge(wo_loaded, 32)
                for j in range(2):
                    ins = nc.scalar.activation(wo[0][:, 4 * j:4 * j + 4, 0:O],
                                               raw_wo[j].rearrange("p (k o) -> p k o", o=O), ACT.Copy)
                ins.then_inc(wo_hi_done, 1)

            one_now, two_now = [True], [True]

            def first_step():
                one_now[0], two_now[0] = True, False
                copy_xt(0, 0), copy_xt(0, 1), split_f(0)
                w_out_hi(), w_heads_hi(), relu_part(0, 0, 0), relu_part(0, 1, 0), exps(0, 0, 0)
                relu_part(0, 0, 1), exps(0, 1, 0), relu_part(0, 1, 1), relu_part(0, 0, 2), exps(0, 0, 1)
                exps(0, 1, 1), pt_hi(0, 0, 0), pt_hi(0, 1, 0), pt_hi(0, 0, 1), relu_part(0, 1, 2)
                exps(0, 0, 2), pt_hi(0, 1, 1), relu_part(0, 0, 3), exps(0, 1, 2), y_hi(0, 0, 0)
                y_hi(0, 1, 0), exps(0, 0, 3), y_hi(0, 0, 1), y_hi(0, 1, 1), relu_part(0, 1, 3)
                pt_hi(0, 0, 2), exps(0, 1, 3), w_exp_(0, 0, 0), copy_xt(1, 0), w_exp_(0, 0, 1)
                w_neg_(0, 0, 0), copy_xt(1, 1), pt_hi(0, 1, 2), w_neg_(0, 0, 1), y_hi(0, 0, 2)
                w_exp_(0, 1, 0), w_neg_(0, 1, 0), pt_hi(0, 0, 3), h_hi(0, 0, 0), pt_hi(0, 1, 3)
                y_hi(0, 1, 2), y_hi(0, 0, 3), w_exp_(0, 1, 1), h_hi(0, 0, 1), y_hi(0, 1, 3), w_neg_(0, 1, 1)
                split_f(1), h_hi(0, 1, 0), w_exp_(0, 2, 0), w_neg_(0, 2, 0), w_exp_(0, 2, 1), h_hi(0, 1, 1)
                w_neg_(0, 2, 1), w_exp_(0, 3, 0), h_hi(0, 2, 0), w_neg_(0, 3, 0), w_exp_(0, 3, 1)
                h_hi(0, 2, 1), h_hi(0, 3, 0), w_neg_(0, 3, 1), h_hi(0, 3, 1)

            def step(p, pre, one, two, post):
                one_now[0], two_now[0] = one, two
                if one:
                    relu_part(p, 0, 0), relu_part(p, 1, 0)
                if two:
                    v_hi_(p, 0, 0)
                if one:
                    relu_part(p, 0, 1), relu_part(p, 1, 1), exps(p, 0, 0), exps(p, 1, 0)
                if two:
                    v_hi_(p, 0, 1)
                if one:
                    exps(p, 0, 1), relu_part(p, 0, 2), relu_part(p, 1, 2), exps(p, 1, 1), pt_hi(p, 0, 0)
                    exps(p, 0, 2)
                if two:
                    split_f2(p, 0)
                if one:
                    pt_hi(p, 1, 0), exps(p, 1, 2), pt_hi(p, 0, 1), relu_part(p, 0, 3)
                if two:
                    v_hi_(p, 1, 0), relu_part(p, 0, H), v_hi_(p, 1, 1)
                if one:
                    y_hi(p, 0, 0), pt_hi(p, 1, 1)
                if two:
                    exps(p, 0, H), split_f2(p, 1)
                if one:
                    y_hi(p, 1, 0), y_hi(p, 0, 1), exps(p, 0, 3), relu_part(p, 1, 3), pt_hi(p, 0, 2)
                if two:
                    relu_part(p, 1, H)
                if pre:
                    copy_xt(p + 1, 0)
                if two:
                    pt_hi(p, 0, H)
                if one:
                    y_hi(p, 1, 1), w_exp_(p, 0, 0), w_neg_(p, 0, 0)
                if two:
                    exps(p, 1, H)
                if one:
                    w_exp_(p, 0, 1), w_neg_(p, 0, 1), pt_hi(p, 1, 2)
                if two:
                    o_exp_(p, 0)
                if one:
                    y_hi(p, 0, 2)
                if two:
                    o_neg_(p, 0), pt_hi(p, 1, H)
                if one:
                    pt_hi(p, 0, 3), exps(p, 1, 3)
                if two:
                    o_hi_(p, 0)
                if one:
                    h_hi(p, 0, 0), w_exp_(p, 1, 0), h_hi(p, 0, 1), w_neg_(p, 1, 0)
                if pre:
                    copy_xt(p + 1, 1)
                if two:
                    o_exp_(p, 1)
                if one:
                    w_exp_(p, 1, 1), y_hi(p, 1, 2), h_hi(p, 1, 0)
                if two:
                    o_neg_(p, 1)
                if one:
                    w_neg_(p, 1, 1), y_hi(p, 0, 3), pt_hi(p, 1, 3)
                if two:
                    o_hi_(p, 1), ffn_relu(p, 0)
                if one:
                    h_hi(p, 1, 1)
                if two:
                    ffn_relu_hi(p, 0)
                if one:
                    w_exp_(p, 2, 0), w_exp_(p, 2, 1)
                if pre:
                    split_f(p + 1)
                if one:
                    w_neg_(p, 2, 0), y_hi(p, 1, 3), w_neg_(p, 2, 1)
                if two:
                    ffn_relu(p, 1), ffn_relu_hi(p, 1)
                if one:
                    h_hi(p, 2, 0), h_hi(p, 2, 1), w_exp_(p, 3, 0), w_neg_(p, 3, 0), w_exp_(p, 3, 1)
                    w_neg_(p, 3, 1), h_hi(p, 3, 0), h_hi(p, 3, 1)

            def last_step():
                one_now[0], two_now[0] = False, True
                v_hi_(PAIRS, 0, 0), v_hi_(PAIRS, 0, 1), split_f2(PAIRS, 0), v_hi_(PAIRS, 1, 0)
                relu_part(PAIRS, 0, H), exps(PAIRS, 0, H), v_hi_(PAIRS, 1, 1), split_f2(PAIRS, 1)
                relu_part(PAIRS, 1, H), pt_hi(PAIRS, 0, H), exps(PAIRS, 1, H), o_exp_(PAIRS, 0)
                pt_hi(PAIRS, 1, H), o_neg_(PAIRS, 0), o_hi_(PAIRS, 0), o_exp_(PAIRS, 1), o_neg_(PAIRS, 1)
                o_hi_(PAIRS, 1), ffn_relu(PAIRS, 0), ffn_relu_hi(PAIRS, 0), ffn_relu(PAIRS, 1)
                ffn_relu_hi(PAIRS, 1)

            for i in range(2):
                half = slice(i * H * O, (i + 1) * H * O)
                act.dma_start(raw_ah[:, half],
                              a_heads.rearrange("h c -> (h c)")[half].partition_broadcast(P)).then_inc(ah_loaded[i], 16)
            act.dma_start(raw_adj.rearrange("p (c m) -> p c m", c=NC),
                          adj.rearrange("(c n) m -> n c m", n=P)).then_inc(adj_loaded, 16)
            act.dma_start(raw_b2, b2.partition_broadcast(2)).then_inc(b2_loaded, 16)
            act.dma_start(b1c[:, :], b1.rearrange("(c p) -> p c", p=P),
                          allow_slow_non_contiguous=True).then_inc(vectors_loaded, 16)
            act.dma_start(gamma_b[:, :], gamma.partition_broadcast(P)).then_inc(vectors_loaded, 16)
            act.dma_start(beta_b[:, :], beta.partition_broadcast(P)).then_inc(vectors_loaded, 16)
            first_step()
            step(1, True, True, True, False)
            with act.Fori(2, PAIRS - 1) as p:
                step(p, True, True, True, True)
            step(PAIRS - 1, False, True, True, True)
            last_step()
            step(PAIRS + 1, False, False, False, True)

        @block.vector
        def _(dve):
            chain = [0]

            def link(ins):
                chain[0] += 1
                ins.then_inc(dve_chain, 1)
                dve.wait_ge(dve_chain, chain[0])

            def set_up():
                for t in (L2, R2, b2r):
                    nc.vector.memset(t[:, :].bitcast(F32), 0.0)
                nc.vector.memset(ones_r[:, :].bitcast(F32), 1.0)
                nc.vector.memset(f2pad[:, :, :, :], 0.0)
                for t in u_in:
                    link(nc.vector.memset(t[:, :, :].bitcast(F32), 0.0))
                dve.wait_ge(consts_made, 1)
                nc.vector.tensor_copy(ident_b[:, :], ident[:, :])
                nc.vector.tensor_copy(ident_r[:, :], ident[:, :])
                link(nc.vector.tensor_reduce(row_w[:, :], row_sel[:, :, :, :].rearrange("p k h e -> p k (h e)"), AX.X,
                                             ALU.add))
                for c in range(FC):
                    dve.wait_ge(wh_loaded[c], 16)
                    for i in range(2 * H):
                        if c == 0 and i % H == 0:
                            dve.wait_ge(ah_loaded[i // H], 16)
                        ins = nc.vector.tensor_tensor_reduce(
                            junk_in[i % 4], raw_wh[c][:, (i // 2) * O:(i // 2 + 1) * O], raw_ah[:, i * O:(i + 1) * O],
                            SLOPE, 0.0, ALU.mult, ALU.add, u_sum[:, c, i:i + 1])
                        if i % 4 == 3:
                            link(ins)
                hi, lo = (t[:, :, :].rearrange("p c (h r) -> p c h r", h=H)[:, :, :, 0:4].rearrange(
                    "p c h (j e) -> p c h j e", e=2) for t in u_in)
                sums = u_sum[:, :, :].rearrange("p c (h j) -> p c h j", j=2)
                for c, e in ((0, 0), (0, 1), (1, 0), (1, 1)):
                    ins = nc.vector.tensor_copy(hi[:, c, :, :, e], sums[:, c, :, :])
                link(ins)
                for c, e in ((0, 0), (0, 1), (1, 0), (1, 1)):
                    ins = nc.vector.tensor_tensor(lo[:, c, :, :, e], sums[:, c, :, :], hi[:, c, :, :, e], ALU.subtract)
                ins.then_inc(u_made, 1)

            def masks_and_bias():
                dve.wait_ge(adj_loaded, 16)
                nc.vector.tensor_scalar(mask[:, :, :].rearrange("p c m -> p (c m)"), raw_adj, 0.0, MASKED,
                                        ALU.is_le, ALU.mult).then_inc(masks_made, 1)
                dve.wait_ge(b2_loaded, 16)
                link(nc.vector.tensor_copy(b2_hi, raw_b2))
                nc.vector.scalar_tensor_tensor(out=b2r[0:2, :], in0=b2_hi, scalar=row_w[0:2, 2:3],
                                               in1=raw_b2, op0=ALU.mult, op1=ALU.add)

            def out_columns(j):
                dve.wait_ge(vectors_loaded, 16 * 4)
                dve.wait_ge(wo_loaded, 32)
                for k in range(4):
                    for i in range(2):
                        ins = nc.vector.tensor_tensor_reduce(junk_out[i], raw_wo[j][:, k * O:(k + 1) * O],
                                                             raw_ao[:, i * O:(i + 1) * O], SLOPE, 0.0, ALU.mult,
                                                             ALU.add, u_out[:, 4 * j + k, i:i + 1])
                    link(ins)

            def split_ffn():
                dve.wait_ge(w12_loaded, 32)
                for i, w in enumerate((w1s, w2s)):
                    ins = nc.vector.tensor_copy(w[0][:, :, :].rearrange("p c o -> p (c o)"),
                                                raw_w12[:, i * OC * O:(i + 1) * OC * O])
                ins.then_inc(w12_hi_done, 1)
                cols = [w[:, :, O:W2N].rearrange("p k (j e) -> p k j e", e=2) for w in wo]
                for e in range(2):
                    ins = nc.vector.tensor_copy(cols[0][:, :, :, e], u_out[:, :, :])
                link(ins)
                dve.wait_ge(wo_lo_done, 2)
                for e in range(2):
                    ins = nc.vector.tensor_tensor(cols[1][:, :, :, e], u_out[:, :, :], cols[0][:, :, :, e], ALU.subtract)
                ins.then_inc(out_made, 1)

            def split_xt(p, b):
                dve.wait_ge(xt_hi_done, p * 2 + b + 1)
                nc.vector.tensor_tensor(xt[1][:, :, b, :], bank[BANK[("xt", b)]][:, :].rearrange(
                    "p (c n) -> p c n", c=FC), xt[0][:, :, b, :], ALU.subtract).then_inc(xt_split, 1)

            def x_hi(p):
                dve.wait_ge(x_loaded, p * 16 + 16)
                reach(dve, y_ready, p * 2 * H)
                nc.vector.tensor_copy(xs[0][:, :, :, :].rearrange("p b c f -> p (b c f)"),
                                      xn[:, :, :, :].rearrange("p b c f -> p (b c f)")).then_inc(x_hi_done, 1)

            def factors(p):
                dve.wait_ge(f_hi_done[0], p + 1)
                reach(dve, lr_done[1], (p - 1) * 2)
                reach(dve, lr_done[0], p)
                nc.vector.scalar_tensor_tensor(out=f_sp[:, :], in0=f_hi[:, :], scalar=row_w[:, 2:3],
                                               in1=bank[BANK[("f",)]][:, :], op0=ALU.mult,
                                               op1=ALU.add).then_inc(f_split[0], 1)
                dve.wait_ge(f_split[0], p + 1)
                reach(dve, z_ready[0], p * 2 * H)
                nc.vector.tensor_scalar(L[:, :], f_sp[:, :], row_w[:, 0:1], row_w[:, 1:2], ALU.mult, ALU.add)
                nc.vector.tensor_scalar(R[:, :], f_sp[:, :], row_w[:, 1:2], row_w[:, 0:1], ALU.mult,
                                        ALU.add).then_inc(lr_done[0], 1)

            def factors2(p, b):
                q = p - 1
                rows, cols = slice(0, 4), slice(b * N, (b + 1) * N)
                dve.wait_ge(f_hi_done[1], q * 2 + b + 1)
                dve.wait_ge(lr_done[0], p + 1 if one_now[0] else PAIRS)
                nc.vector.scalar_tensor_tensor(out=f_sp[rows, cols], in0=f_hi[rows, cols], scalar=row_w[rows, 2:3],
                                               in1=bank[BANK[("f2", b)]][rows, 0:N], op0=ALU.mult,
                                               op1=ALU.add).then_inc(f_split[1], 1)
                dve.wait_ge(f_split[1], q * 2 + b + 1)
                reach(dve, z_ready[1], q * 2)
                nc.vector.tensor_scalar(L2[rows, cols], f_sp[rows, cols], row_w[rows, 0:1], row_w[rows, 1:2],
                                        ALU.mult, ALU.add)
                nc.vector.tensor_scalar(R2[rows, cols], f_sp[rows, cols], row_w[rows, 1:2], row_w[rows, 0:1],
                                        ALU.mult, ALU.add).then_inc(lr_done[1], 1)

            def logits(p, b, h):
                ly, s = layer_of(h), att_slot(h)
                reach_alone(dve, (u_made, 1), (relu_done[ly], item(ly, p - ly, b, h)))
                ps = bank[BANK[("z", b, h)]]
                for c in range(NC):
                    ins = nc.vector.tensor_tensor_reduce(att[:, s, b, c, :], ps[:, c * N:(c + 1) * N],
                                                         att[:, s, b, c, :], -1.0, 3.0e38, ALU.add, ALU.min,
                                                         negmax[:, s, b, c:c + 1])
                ins.then_inc(logits_done[ly], 1)

            def normalize(p, b, h):
                ly, s = layer_of(h), att_slot(h)
                n = item(ly, p - ly, b, h)
                dve.wait_ge(exp_done[ly], n)
                nc.vector.reciprocal(inv[:, s, b, :], total[:, s, b, :]).then_inc(inv_done[ly], 1)
                dve.wait_ge(inv_done[ly], n)
                for c in range(NC):
                    ins = nc.vector.tensor_scalar(att[:, s, b, c, :], att[:, s, b, c, :], inv[:, s, b, c:c + 1], None,
                                                  ALU.mult)
                ins.then_inc(probs_done[ly], 1)

            def pt_lo(p, b, h):
                ly = layer_of(h)
                dve.wait_ge(pt_hi_done[ly], item(ly, p - ly, b, h))
                dst = [t[:, pt_slot(h), b, :, :].rearrange("p c n -> p (c n)") for t in pt]
                nc.vector.tensor_tensor(dst[1], bank[BANK[("t", b, h)]][:, :], dst[0],
                                        ALU.subtract).then_inc(pt_lo_done[ly], 1)

            def y_lo(p, b, h):
                dve.wait_ge(y_hi_done, item(0, p, b, h))
                nc.vector.tensor_tensor(yt[1][:, h % 2, :, b, :], bank[BANK[("y", b, h)]][:, :].rearrange(
                    "p (c n) -> p c n", c=FC), yt[0][:, h % 2, :, b, :], ALU.subtract).then_inc(y_lo_done, 1)

            def elu(p, h, oc):
                i = OC * h + oc
                dve.wait_ge(w_neg, p * KC + i + 1)
                nc.vector.scalar_tensor_tensor(out=elu_w[:, i % 4, :], in0=bank[BANK[("w", h, oc)]][:, :], scalar=0.0,
                                               in1=elu_w[:, i % 4, :], op0=ALU.max, op1=ALU.subtract).then_inc(w_elu, 1)

            def v_lo_(p, b, mc):
                dve.wait_ge(v_hi, (p - 1) * 4 + 2 * b + mc + 1)
                dve.wait_ge(f2_cols, (p - 1) * 4 + 2 * b + mc + 1)
                nc.vector.tensor_tensor(v[1][:, b, mc, :], bank[BANK[("v", b, mc)]][:, 0:O], v[0][:, b, mc, :],
                                        ALU.subtract).then_inc(v_lo, 1)

            def elu_out(p, b):
                q = p - 1
                dve.wait_ge(o_neg, q * 2 + b + 1)
                nc.vector.scalar_tensor_tensor(out=graph(elu_o, b), in0=halves(bank[BANK[("o", b)]]), scalar=0.0,
                                               in1=graph(elu_o, b), op0=ALU.max, op1=ALU.subtract).then_inc(o_elu, 1)

            def norm_stats(p, b):
                q = p - 1
                n = q * 2 + b + 1
                ps = bank[BANK[("r", b)]]
                dve.wait_ge(r_ready, n)
                for c in range(NC):
                    ins = nc.vector.bn_stats(bn1[:, b, c, :], ps[:, c * O:(c + 1) * O])
                ins.then_inc(bn1_done, 1)
                reach_alone(dve, (u_made, 1), (bn1_done, n))
                for c in range(NC):
                    ins = nc.vector.bn_aggr(mv1[:, b, c, :], bn1[:, b, c, :])
                ins.then_inc(mv1_done, 1)
                dve.wait_ge(mv1_done, n)
                reach(dve, stored, q * 32)
                for c in range(NC):
                    ins = nc.vector.scalar_tensor_tensor(out=ln[:, b, c, :], in0=ps[:, c * O:(c + 1) * O],
                                                         scalar=mv1[:, b, c, 0:1], in1=gamma_b[:, :],
                                                         op0=ALU.subtract, op1=ALU.mult)
                ins.then_inc(scaled, 1)

            def add_residual(p, b):
                q = p - 1
                n = q * 2 + b + 1
                dve.wait_ge(rs1_done, n)
                dve.wait_ge(scaled, n)
                dve.wait_ge(xres_ready, q + 1)
                for c in range(NC):
                    ins = nc.vector.scalar_tensor_tensor(out=ln[:, b, c, :], in0=ln[:, b, c, :],
                                                         scalar=rs1[:, b, c:c + 1], in1=xres[:, b, c, :],
                                                         op0=ALU.mult, op1=ALU.add)
                ins.then_inc(ln1_done, 1)
                dve.wait_ge(ln1_done, n)
                for c in range(NC):
                    ins = nc.vector.bn_stats(bn2[:, b, c, :], ln[:, b, c, :])
                ins.then_inc(bn2_done, 1)
                reach_alone(dve, (u_made, 1), (bn2_done, n))
                for c in range(NC):
                    ins = nc.vector.bn_aggr(mv2[:, b, c, :], bn2[:, b, c, :])
                ins.then_inc(mv2_done, 1)

            def second_norm(p, b):
                n = (p - 1) * 2 + b + 1
                dve.wait_ge(rs2_done, n)
                for c in range(NC):
                    ins = nc.vector.tensor_scalar(ln[:, b, c, :], ln[:, b, c, :], mv2[:, b, c, 0:1],
                                                  rs2[:, b, c:c + 1], ALU.subtract, ALU.mult)
                ins.then_inc(ln2_done, 1)

            one_now = [True]

            def first_step():
                one_now[0] = True
                split_xt(0, 0), split_xt(0, 1), masks_and_bias(), factors(0)
                x_hi(0), logits(0, 0, 0), logits(0, 1, 0), normalize(0, 0, 0), logits(0, 0, 1)
                normalize(0, 1, 0), logits(0, 1, 1), logits(0, 0, 2), normalize(0, 0, 1), normalize(0, 1, 1)
                pt_lo(0, 0, 0), pt_lo(0, 1, 0), pt_lo(0, 0, 1), logits(0, 1, 2), normalize(0, 0, 2)
                pt_lo(0, 1, 1), logits(0, 0, 3), normalize(0, 1, 2), y_lo(0, 0, 0), y_lo(0, 1, 0)
                normalize(0, 0, 3), y_lo(0, 0, 1), y_lo(0, 1, 1), logits(0, 1, 3), pt_lo(0, 0, 2)
                out_columns(0), split_xt(1, 0), normalize(0, 1, 3), elu(0, 0, 0), pt_lo(0, 1, 2)
                elu(0, 0, 1), split_xt(1, 1), pt_lo(0, 0, 3), elu(0, 1, 0), pt_lo(0, 1, 3), y_lo(0, 0, 2)
                y_lo(0, 1, 2), out_columns(1), y_lo(0, 0, 3), y_lo(0, 1, 3), elu(0, 1, 1), elu(0, 2, 0)
                factors(1), elu(0, 2, 1), elu(0, 3, 0), split_ffn(), elu(0, 3, 1)

            def step(p, pre, one, two, post):
                one_now[0] = one
                if one:
                    logits(p, 0, 0), logits(p, 1, 0)
                if post:
                    add_residual(p - 1, 0)
                if one:
                    logits(p, 0, 1), x_hi(p), normalize(p, 0, 0), logits(p, 1, 1), normalize(p, 1, 0)
                    normalize(p, 0, 1), logits(p, 0, 2), logits(p, 1, 2)
                if two:
                    v_lo_(p, 0, 0)
                if one:
                    pt_lo(p, 0, 0)
                if two:
                    v_lo_(p, 0, 1), factors2(p, 0)
                if one:
                    pt_lo(p, 1, 0), normalize(p, 1, 1), pt_lo(p, 0, 1), logits(p, 0, 3)
                if two:
                    v_lo_(p, 1, 0), logits(p, 0, H), v_lo_(p, 1, 1)
                if one:
                    normalize(p, 0, 2), pt_lo(p, 1, 1), y_lo(p, 0, 0)
                if two:
                    factors2(p, 1)
                if one:
                    y_lo(p, 1, 0), normalize(p, 1, 2)
                if two:
                    normalize(p, 0, H)
                if one:
                    y_lo(p, 0, 1), logits(p, 1, 3)
                if two:
                    logits(p, 1, H), pt_lo(p, 0, H)
                if one:
                    pt_lo(p, 0, 2)
                if pre:
                    split_xt(p + 1, 0)
                if one:
                    elu(p, 0, 0), y_lo(p, 1, 1), normalize(p, 0, 3)
                if two:
                    normalize(p, 1, H)
                if one:
                    pt_lo(p, 1, 2), y_lo(p, 0, 2), elu(p, 0, 1)
                if two:
                    pt_lo(p, 1, H), elu_out(p, 0)
                if one:
                    pt_lo(p, 0, 3), normalize(p, 1, 3)
                if post:
                    add_residual(p - 1, 1)
                if one:
                    elu(p, 1, 0), y_lo(p, 1, 2)
                if two:
                    elu_out(p, 1)
                if pre:
                    split_xt(p + 1, 1)
                if one:
                    y_lo(p, 0, 3), elu(p, 1, 1), pt_lo(p, 1, 3)
                if post:
                    second_norm(p - 1, 0), second_norm(p - 1, 1)
                if pre:
                    factors(p + 1)
                if one:
                    y_lo(p, 1, 3), elu(p, 2, 0), elu(p, 2, 1)
                if two:
                    norm_stats(p, 0)
                if one:
                    elu(p, 3, 0), elu(p, 3, 1)
                if two:
                    norm_stats(p, 1)

            def last_step():
                one_now[0] = False
                add_residual(PAIRS - 1, 0), v_lo_(PAIRS, 0, 0), v_lo_(PAIRS, 0, 1), factors2(PAIRS, 0)
                logits(PAIRS, 0, H), v_lo_(PAIRS, 1, 0), normalize(PAIRS, 0, H), v_lo_(PAIRS, 1, 1)
                factors2(PAIRS, 1), second_norm(PAIRS - 1, 0), logits(PAIRS, 1, H), pt_lo(PAIRS, 0, H)
                normalize(PAIRS, 1, H), pt_lo(PAIRS, 1, H), elu_out(PAIRS, 0), elu_out(PAIRS, 1)
                add_residual(PAIRS - 1, 1), second_norm(PAIRS - 1, 1), norm_stats(PAIRS, 0)
                norm_stats(PAIRS, 1)

            set_up()
            first_step()
            step(1, True, True, True, False)
            with dve.Fori(2, PAIRS - 1) as p:
                step(p, True, True, True, True)
            step(PAIRS - 1, False, True, True, True)
            last_step()
            step(PAIRS + 1, False, False, False, True)


_INS = ['x', 'adj', 'L0_gnn_W_heads', 'L0_gnn_a_heads', 'L0_gnn_W_out', 'L0_gnn_a_out', 'L0_gnn_w1', 'L0_gnn_b1',
        'L0_gnn_w2', 'L0_gnn_b2', 'L0_gnn_ln_gamma', 'L0_gnn_ln_beta']
_OUTS = [((32, 256, 256), 'float32')]


def kernel(**inputs):
    import numpy as _np
    import concourse.bacc as _bacc
    from concourse import mybir as _mybir
    from concourse.bass_utils import run_bass_kernel_spmd as _run

    nc = _bacc.Bacc("TRN2", target_bir_lowering=False, num_devices=1)
    arrays, args = {}, []
    for name in _INS:
        a = _np.ascontiguousarray(inputs[name])
        arrays[f"in_{name}_dram"] = a
        args.append(nc.dram_tensor(f"in_{name}_dram", a.shape, _mybir.dt.from_np(a.dtype), kind="ExternalInput").ap())
    for i, (shape, dtype) in enumerate(_OUTS):
        dt = _mybir.dt.from_np(_np.dtype(dtype))
        args.append(nc.dram_tensor(f"out_{i}_dram", shape, dt, kind="ExternalOutput").ap())
    gat_block(nc, *args)
    r = _run(nc, [arrays], core_ids=[0])
    got = tuple(r.results[0][f"out_{i}_dram"] for i in range(len(_OUTS)))
    return got[0]
```
